# Optimizing a Trainium2 kernel written in Bass

```python
import numpy as np
import jax
import jax.numpy as jnp

def _softmax(x, axis=-1):
    return jax.nn.softmax(x, axis=axis)
def _gelu(x):
    return jax.nn.gelu(x, approximate=True)
def _silu(x):
    return jax.nn.silu(x)
def _sigmoid(x):
    return jax.nn.sigmoid(x)
def _layernorm(x, axis=-1, eps=1e-5):
    m = jnp.mean(x, axis=axis, keepdims=True)
    v = jnp.var(x, axis=axis, keepdims=True)
    return (x - m) / jnp.sqrt(v + eps)
def _scatter_add(tgt, idx, src, axis=0):
    return tgt.at[idx].add(src)
def _segment_sum(src, seg, n):
    return jax.ops.segment_sum(src, seg, n)

kernel_name = 'mk_conv_seq_d2_conv_nchw64_80d3bd'

def setup_inputs(seed: int = 0):
    np.random.seed(seed)
    _w = jnp.asarray
    def _rec_inputs():
        import jax
        import jax.numpy as jnp
        _gk = jax.random.key(seed)
        x = -0.0003929 + 0.9999 * jax.random.normal(jax.random.fold_in(_gk, 1), (16, 64, 128, 128), jnp.float32)
        return x
    x = _rec_inputs()
    def _L0_conv_setup():
        import jax, jax.numpy as jnp
        import numpy as np
        from jax import lax
        CUTOFF = 0.25
        SIGMA = 1.0
        RADIUS = 4

        def _gauss_kernel(sigma=SIGMA, radius=RADIUS):
            x = np.arange(-radius, radius + 1, dtype=np.float32)
            k = np.exp(-0.5 * (x / sigma) ** 2)
            return jnp.asarray(k / k.sum())

        def _blur_axis(x, axis, kernel):
            r = (kernel.shape[0] - 1) // 2
            pad = [(0, 0)] * x.ndim
            pad[axis] = (r, r)
            xp = jnp.pad(x, pad, mode='edge')
            out = jnp.zeros_like(x)
            for i in range(kernel.shape[0]):
                out = out + kernel[i] * lax.slice_in_dim(xp, i, i + x.shape[axis], axis=axis)
            return out

        def gaussian_smoothing_4d(x):
            k = _gauss_kernel().astype(x.dtype)
            for ax in range(4):
                x = _blur_axis(x, ax, k)
            return x

        def dht_2d(x):
            return (jnp.fft.fftn(x, axes=(2, 3)).real - jnp.fft.fftn(jnp.flip(x, axis=(2, 3)), axes=(2, 3)).imag).astype(x.dtype)

        def _neg_k(a):
            return jnp.roll(jnp.flip(a, axis=(-2, -1)), shift=(1, 1), axis=(-2, -1))

        def compl_mul2d(x1, x2):
            x1n, x2n = (_neg_k(x1), _neg_k(x2))
            e = lambda a, b: jnp.einsum('bixy,ioxy->boxy', a, b)
            return 0.5 * (e(x1, x2) - e(x1n, x2n) + e(x1, x2n) + e(x1n, x2))
        key = jax.random.key(seed)
        k1, k2 = jax.random.split(key)
        B, Cin, Cout, H, W, M1, M2 = (16, 64, 64, 128, 128, 20, 20)
        x = jax.random.normal(k1, (B, Cin, H, W), dtype=jnp.float32)
        scale = 1.0 / (Cin * Cout)
        w1 = scale * jax.random.uniform(k2, (Cin, Cout, M1, M2), dtype=jnp.float32)
        return {'x': x, 'w1': w1}
    _L0_conv_all = _L0_conv_setup()
    _L0_conv_in = {k: v for k, v in _L0_conv_all.items() if k in ('w1', )}
    del _L0_conv_all

    def _L1_conv_setup():
        import jax, jax.numpy as jnp
        import numpy as np
        EPS = 1e-05

        def _bn(x, g, b, m, v):
            scale = g * jax.lax.rsqrt(v + EPS)
            return x * scale[None, :, None, None] + (b - m * scale)[None, :, None, None]

        def _prelu(x, a):
            return jnp.where(x >= 0, x, a[None, :, None, None] * x)

        def _conv3x3(x, w):
            return jax.lax.conv_general_dilated(x, w, window_strides=(1, 1), padding=((1, 1), (1, 1)), dimension_numbers=('NCHW', 'OIHW', 'NCHW'))
        key = jax.random.key(seed)
        ks = jax.random.split(key, 16)
        B, C, H, W = (64, 64, 112, 112)
        x = jax.random.normal(ks[0], (B, C, H, W), jnp.float32)
        w1 = jax.random.normal(ks[1], (C, C, 3, 3), jnp.float32) * 0.05
        w2 = jax.random.normal(ks[2], (C, C, 3, 3), jnp.float32) * 0.05

        def bn_params(k):
            k1, k2, k3, k4 = jax.random.split(k, 4)
            g = 1.0 + 0.1 * jax.random.normal(k1, (C,), jnp.float32)
            b = 0.1 * jax.random.normal(k2, (C,), jnp.float32)
            m = 0.1 * jax.random.normal(k3, (C,), jnp.float32)
            v = jax.random.uniform(k4, (C,), jnp.float32, 0.5, 1.5)
            return (g, b, m, v)
        bn0_g, bn0_b, bn0_m, bn0_v = bn_params(ks[3])
        bn1_g, bn1_b, bn1_m, bn1_v = bn_params(ks[4])
        bn2_g, bn2_b, bn2_m, bn2_v = bn_params(ks[5])
        prelu1_a = jnp.full((C,), 0.25, jnp.float32)
        prelu2_a = jnp.full((C,), 0.25, jnp.float32)
        return {'x': x, 'w1': w1, 'w2': w2, 'bn0_g': bn0_g, 'bn0_b': bn0_b, 'bn0_m': bn0_m, 'bn0_v': bn0_v, 'bn1_g': bn1_g, 'bn1_b': bn1_b, 'bn1_m': bn1_m, 'bn1_v': bn1_v, 'bn2_g': bn2_g, 'bn2_b': bn2_b, 'bn2_m': bn2_m, 'bn2_v': bn2_v, 'prelu1_a': prelu1_a, 'prelu2_a': prelu2_a}
    _L1_conv_all = _L1_conv_setup()
    _L1_conv_in = {k: v for k, v in _L1_conv_all.items() if k in ('w1', 'w2', 'bn0_g', 'bn0_b', 'bn0_m', 'bn0_v', 'bn1_g', 'bn1_b', 'bn1_m', 'bn1_v', 'bn2_g', 'bn2_b', 'bn2_m', 'bn2_v', 'prelu1_a', 'prelu2_a', )}
    del _L1_conv_all

    return {
        "x": x,
        "L0_conv_w1": _L0_conv_in["w1"],
        "L1_conv_w1": _L1_conv_in["w1"],
        "L1_conv_w2": _L1_conv_in["w2"],
        "L1_conv_bn0_g": _L1_conv_in["bn0_g"],
        "L1_conv_bn0_b": _L1_conv_in["bn0_b"],
        "L1_conv_bn0_m": _L1_conv_in["bn0_m"],
        "L1_conv_bn0_v": _L1_conv_in["bn0_v"],
        "L1_conv_bn1_g": _L1_conv_in["bn1_g"],
        "L1_conv_bn1_b": _L1_conv_in["bn1_b"],
        "L1_conv_bn1_m": _L1_conv_in["bn1_m"],
        "L1_conv_bn1_v": _L1_conv_in["bn1_v"],
        "L1_conv_bn2_g": _L1_conv_in["bn2_g"],
        "L1_conv_bn2_b": _L1_conv_in["bn2_b"],
        "L1_conv_bn2_m": _L1_conv_in["bn2_m"],
        "L1_conv_bn2_v": _L1_conv_in["bn2_v"],
        "L1_conv_prelu1_a": _L1_conv_in["prelu1_a"],
        "L1_conv_prelu2_a": _L1_conv_in["prelu2_a"],
    }

def reference(x, L0_conv_w1, L1_conv_w1, L1_conv_w2, L1_conv_bn0_g, L1_conv_bn0_b, L1_conv_bn0_m, L1_conv_bn0_v, L1_conv_bn1_g, L1_conv_bn1_b, L1_conv_bn1_m, L1_conv_bn1_v, L1_conv_bn2_g, L1_conv_bn2_b, L1_conv_bn2_m, L1_conv_bn2_v, L1_conv_prelu1_a, L1_conv_prelu2_a):
    import jax
    import jax.numpy as jnp
    def _L0_conv_ref(x, w1):
        import jax, jax.numpy as jnp
        import numpy as np
        from jax import lax
        CUTOFF = 0.25
        SIGMA = 1.0
        RADIUS = 4

        def _gauss_kernel(sigma=SIGMA, radius=RADIUS):
            x = np.arange(-radius, radius + 1, dtype=np.float32)
            k = np.exp(-0.5 * (x / sigma) ** 2)
            return jnp.asarray(k / k.sum())

        def _blur_axis(x, axis, kernel):
            r = (kernel.shape[0] - 1) // 2
            pad = [(0, 0)] * x.ndim
            pad[axis] = (r, r)
            xp = jnp.pad(x, pad, mode='edge')
            out = jnp.zeros_like(x)
            for i in range(kernel.shape[0]):
                out = out + kernel[i] * lax.slice_in_dim(xp, i, i + x.shape[axis], axis=axis)
            return out

        def gaussian_smoothing_4d(x):
            k = _gauss_kernel().astype(x.dtype)
            for ax in range(4):
                x = _blur_axis(x, ax, k)
            return x

        def dht_2d(x):
            return (jnp.fft.fftn(x, axes=(2, 3)).real - jnp.fft.fftn(jnp.flip(x, axis=(2, 3)), axes=(2, 3)).imag).astype(x.dtype)

        def _neg_k(a):
            return jnp.roll(jnp.flip(a, axis=(-2, -1)), shift=(1, 1), axis=(-2, -1))

        def compl_mul2d(x1, x2):
            x1n, x2n = (_neg_k(x1), _neg_k(x2))
            e = lambda a, b: jnp.einsum('bixy,ioxy->boxy', a, b)
            return 0.5 * (e(x1, x2) - e(x1n, x2n) + e(x1, x2n) + e(x1n, x2))
        B, _, H, W = x.shape
        Cout, M1, M2 = (w1.shape[1], w1.shape[2], w1.shape[3])
        x_ht = dht_2d(x)
        out_ht = jnp.zeros((B, Cout, H, W), dtype=x.dtype)
        out_ht = out_ht.at[:, :, :M1, :M2].set(compl_mul2d(x_ht[:, :, :M1, :M2], w1))
        y = dht_2d(out_ht) / (H * W)
        y = gaussian_smoothing_4d(y)
        freqs = jnp.fft.fftfreq(W)
        mask = (jnp.abs(freqs) <= CUTOFF).astype(y.dtype)
        return y * mask

    def _L1_conv_ref(x, w1, w2, bn0_g, bn0_b, bn0_m, bn0_v, bn1_g, bn1_b, bn1_m, bn1_v, bn2_g, bn2_b, bn2_m, bn2_v, prelu1_a, prelu2_a):
        import jax, jax.numpy as jnp
        import numpy as np
        EPS = 1e-05

        def _bn(x, g, b, m, v):
            scale = g * jax.lax.rsqrt(v + EPS)
            return x * scale[None, :, None, None] + (b - m * scale)[None, :, None, None]

        def _prelu(x, a):
            return jnp.where(x >= 0, x, a[None, :, None, None] * x)

        def _conv3x3(x, w):
            return jax.lax.conv_general_dilated(x, w, window_strides=(1, 1), padding=((1, 1), (1, 1)), dimension_numbers=('NCHW', 'OIHW', 'NCHW'))
        out = _bn(x, bn0_g, bn0_b, bn0_m, bn0_v)
        out = _conv3x3(out, w1)
        out = _bn(out, bn1_g, bn1_b, bn1_m, bn1_v)
        out = _prelu(out, prelu1_a)
        out = _conv3x3(out, w2)
        out = _bn(out, bn2_g, bn2_b, bn2_m, bn2_v)
        out = out + x
        out = _prelu(out, prelu2_a)
        return out

    def _gn(v, G=32, eps=1e-5):
        B_, C_, H_, W_ = v.shape
        g = v.reshape(B_, G, C_ // G, H_, W_)
        m = jnp.mean(g, axis=(2, 3, 4), keepdims=True)
        s = jnp.var(g, axis=(2, 3, 4), keepdims=True)
        return ((g - m) / jnp.sqrt(s + eps)).reshape(v.shape)

    def _ln_c(v, eps=1e-6):
        m = jnp.mean(v, axis=1, keepdims=True)
        s = jnp.var(v, axis=1, keepdims=True)
        return (v - m) / jnp.sqrt(s + eps)

    def _ln_t(v, eps=1e-5):
        m = jnp.mean(v, axis=-1, keepdims=True)
        s = jnp.var(v, axis=-1, keepdims=True)
        return (v - m) / jnp.sqrt(s + eps)

    def _to_tokens(v):
        B_, C_, H_, W_ = v.shape
        return v.reshape(B_, C_, H_ * W_).transpose(0, 2, 1)
    def _from_tokens(t, like):
        B_, C_, H_, W_ = like.shape
        return t.transpose(0, 2, 1).reshape(B_, C_, H_, W_)

    x = _L0_conv_ref(x, L0_conv_w1)
    x = _L1_conv_ref(x, L1_conv_w1, L1_conv_w2, L1_conv_bn0_g, L1_conv_bn0_b, L1_conv_bn0_m, L1_conv_bn0_v, L1_conv_bn1_g, L1_conv_bn1_b, L1_conv_bn1_m, L1_conv_bn1_v, L1_conv_bn2_g, L1_conv_bn2_b, L1_conv_bn2_m, L1_conv_bn2_v, L1_conv_prelu1_a, L1_conv_prelu2_a)
    return x


_drawn_inputs = setup_inputs


def setup_inputs(seed=0):
    import zlib

    import numpy as np

    out = dict(_drawn_inputs(seed))
    spreads = {'L1_conv_prelu1_a': (0.25, 0.2), 'L1_conv_prelu2_a': (0.25, 0.2)}
    factors = {'x': 32.269, 'L0_conv_w1': 64.0}
    for name, (base, spread) in spreads.items():
        noise = np.random.default_rng([zlib.crc32(name.encode()), seed]).standard_normal(out[name].shape)
        drawn = base * np.exp(spread * noise) if base else spread * noise
        out[name] = jnp.asarray(drawn.astype(out[name].dtype))
    for name, factor in factors.items():
        out[name] = (out[name] * factor).astype(out[name].dtype)
    return out
```

```python
from contextlib import ExitStack

import concourse.bass as bass
from concourse import mybir

ACT = mybir.ActivationFunctionType
ALU = mybir.AluOpType
F32 = mybir.dt.float32
F32R = mybir.dt.float32r

B, C, N, K = 16, 64, 128, 20
BP = B // 2
KE = K + 1
NF = 2 * K
NP = 2 * (K + 1)
NM = K * K
WLO, WHI = 33, 96
R = 4
EPS = 1e-5

CH = 16
XR = 4
CPP = 2 * C // CH
GI = 8
GPP = 2 * C // GI
MC = 25
NMC = NM // MC
WR = 8
MT = 100

NE = 38
E0, E1, EPAD = 2, 36, 18
NEY = E1 - E0
NO = 36
G = 9
ZK = 3
JB = 7
HP = N + 2
MID0, MID1 = 36, 94


def conv_seq_kernel(nc, x, wmix, wconv, pcol, prow, fwd, f2tab, bblur, cblur, ytab, lift, ident, out):
    xs = x.rearrange("b (n i) h w -> (b n) h i w", i=CH)
    modes = nc.dram_tensor("modes", (B, NM, C), F32, kind="Internal").ap()

    with ExitStack() as ctx:
        def sem(name):
            return ctx.enter_context(nc.semaphore(name))

        def sb(name, shape, dt=F32, stack=ctx):
            return stack.enter_context(nc.sbuf_tensor(name, shape, dt))

        bank = ctx.enter_context(nc.psum_tensor("bank", [128, 8, 512], F32))

        ident_sb = sb("ident_sb", [128, 128])
        ytab_sb = sb("ytab_sb", [4 * K, 2 * NEY])
        lift_sb = sb("lift_sb", [3 * NP, N])
        rowfun_sb = sb("rowfun_sb", [NP, N])
        pcol_sb = sb("pcol_sb", [128, 14])
        coef = sb("coef", [128, 16])
        w_hi = [sb(f"w_hi{l}", [128, 6, 128], F32R) for l in range(2)]
        w_lo = [sb(f"w_lo{l}", [128, 6, 128], F32R) for l in range(2)]
        yin = sb("yin", [4 * K, KE, 128])
        u = sb("u", [128, NE, NP])
        yr = sb("yr", [128, NE, NP])
        first = ExitStack()
        bblur_sb = sb("bblur_sb", [128, 5, 128], stack=first)
        fwd_sb = sb("fwd_sb", [128, NF], stack=first)
        f2_sb = sb("f2_sb", [128, 2, KE, KE], stack=first)
        cblur_sb = sb("cblur_sb", [C, C], stack=first)
        prow_sb = sb("prow_sb", [128, 4, 128], stack=first)
        w_f = sb("w_f", [128, 2, 6, 128], stack=first)
        var, inv, root = (sb(n, [128, 3 + 2 * 128], stack=first) for n in ("var", "inv", "root"))
        xbuf = sb("xbuf", [128, XR, CH, N], stack=first)
        tbuf = sb("tbuf", [128, 2 * C, NF], stack=first)
        hbuf = sb("hbuf", [128, BP + 4, KE * KE], stack=first)
        hblur = sb("hblur", [128, KE, KE], stack=first)
        xx = sb("xx", [128, NM, B], stack=first)
        wbuf = sb("wbuf", [128, WR, MC, C], stack=first)
        mixed = xbuf[0:C].rearrange("p r i w -> p (r i w)")[:, 0:B * NM].rearrange("p (b m) -> p b m", b=B)
        turned = tbuf[0:MT].rearrange("p i f -> p (i f)")[:, 0:4 * B * C].rearrange("p (g b c) -> p g b c", g=4, b=B)
        first.close()
        u_hi = sb("u_hi", [128, NE, NP], F32R)
        u_lo = sb("u_lo", [128, NE, NP], F32R)
        z = sb("z", [128, NO, 3 * NP])
        zt = sb("zt", [3 * NP, 3, 512])
        yt = sb("yt", [NP, G, 512])
        neg = sb("neg", [128, 3, 512])
        act_f = sb("act_f", [128, 3, 512])
        a_hi = sb("a_hi", [128, NO + 1, HP], F32R)
        a_lo = sb("a_lo", [128, NO + 1, HP], F32R)
        obuf = sb("obuf", [128, 2, C, N])

        consts_in = sem("consts_in")
        x_in = [sem(f"x_in{s}") for s in range(XR)]
        rows_full = sem("rows_full")
        rows_out = sem("rows_out")
        modes_full = sem("modes_full")
        modes_out = sem("modes_out")
        edges = sem("edges")
        blur_full = sem("blur_full")
        blur_out = sem("blur_out")
        xx_ready = sem("xx_ready")
        w_in = [sem(f"w_in{s}") for s in range(WR)]
        mix_full = sem("mix_full")
        mix_out = sem("mix_out")
        turn_full = sem("turn_full")
        turn_out = sem("turn_out")
        modes_stored = sem("modes_stored")
        chain = sem("chain")
        zeroed = sem("zeroed")
        w_split = sem("w_split")
        inv_ready = sem("inv_ready")
        root_ready = sem("root_ready")
        coef_ready = sem("coef_ready")
        u_static = sem("u_static")
        yin_in = sem("yin_in")
        y_full = sem("y_full")
        u_out = sem("u_out")
        yr_out = sem("yr_out")
        u_hi_ready = sem("u_hi_ready")
        u_lo_ready = sem("u_lo_ready")
        z_full = sem("z_full")
        z_out = sem("z_out")
        zt_full = sem("zt_full")
        zt_out = sem("zt_out")
        yt_full = sem("yt_full")
        yt_out = sem("yt_out")
        z1_full = sem("z1_full")
        neg1_ready = sem("neg1_ready")
        act_ready = sem("act_ready")
        a_hi_ready = sem("a_hi_ready")
        a_lo_ready = sem("a_lo_ready")
        conv_full = sem("conv_full")
        neg2_ready = sem("neg2_ready")
        cols_out = sem("cols_out")
        mid_ready = sem("mid_ready")
        stored = sem("stored")

        S0, SH0, B1, B2, C1, C2 = (coef[:, i:i + 1] for i in range(6))
        NC_CONST = 11

        block = ctx.enter_context(nc.Block())

        @block.sync
        def _(sp):
            def load_x(n, s):
                for half in range(2):
                    rows = slice(half * CH // 2, (half + 1) * CH // 2)
                    sp.dma_start(xbuf[:, s, rows], xs[n][:, rows]).then_inc(x_in[s], 16)

            for dst, src in ((fwd_sb[:, :], fwd),):
                sp.dma_start(dst, src).then_inc(consts_in, 16)
            for s in range(XR):
                load_x(s, s)
            for dst, src in ((f2_sb[:, :, :, :], f2tab), (bblur_sb[:, :, :], bblur),
                             (cblur_sb[:, :], cblur), (ytab_sb[:, :], ytab), (lift_sb[:, :], lift),
                             (rowfun_sb[:, :], lift[NP:2 * NP, :]), (ident_sb[:, :], ident),
                             (pcol_sb[:, :], pcol), (prow_sb[:, :, :], prow), (w_f[:, :, :, :], wconv)):
                sp.dma_start(dst, src).then_inc(consts_in, 16)
            with sp.Fori(1, B * C // CH // XR) as r:
                for s in range(XR):
                    sp.wait_ge(rows_full, ((r - 1) * XR + s + 1) * (CH // GI))
                    load_x(r * XR + s, s)
            for g in range(4):
                sp.wait_ge(turn_out, 2 * g + 2)
                sp.dma_start(modes[:, g * MT:(g + 1) * MT, :].rearrange("b m c -> m b c"),
                             turned[:, g]).then_inc(modes_stored, 16)
            sp.wait_ge(modes_stored, 64)
            sp.wait_ge(zeroed, 1)

            def load_yin(b):
                src = modes[b].rearrange("(i j) c -> j i c", i=K)
                for q in range(4):
                    shift, par = q % 2, q // 2
                    sp.dma_start(yin[q * K:(q + 1) * K, shift:shift + K, par * C:(par + 1) * C],
                                 src).then_inc(yin_in, 16)

            def store(b, masked):
                sp.wait_ge(cols_out, G * b + 2 * G)
                sp.wait_ge(mid_ready, masked)
                sp.wait_ge(stored, 16 * b + 32)
                sp.dma_start(out[b].rearrange("c (t h) w -> t c (h w)", t=2),
                             obuf[:, b % 2].rearrange("p h w -> p (h w)")).then_inc(stored, 16)

            load_yin(0)
            for b in range(2):
                sp.wait_ge(y_full, 3 * (b + 1))
                load_yin(b + 1)
                store(b, b + 1)
            with sp.Fori(2, B - 1) as b:
                sp.wait_ge(y_full, 3 * (b + 1))
                load_yin(b + 1)
                store(b, 2)
            store(B - 1, 2)
            sp.wait_ge(stored, 16 * (B + 2))

        @block.gpsimd
        def _(pool):
            pool.memset(yin[:, :, :], 0.0).then_inc(zeroed, 1)
            pool.wait_ge(modes_out, 4)
            for s in range(WR):
                pool.dma_start(wbuf[:, s], wmix[:, s * MC:(s + 1) * MC, :]).then_inc(w_in[s], 16)
            for s in range(WR):
                pool.wait_ge(mix_full, s + 1)
                pool.dma_start(wbuf[:, s], wmix[:, (s + WR) * MC:(s + WR + 1) * MC, :]).then_inc(w_in[s], 16)
            for b in range(2):
                pool.wait_ge(cols_out, G * (b + 2))
                pool.tensor_copy(obuf[:, b, :, MID0:MID1],
                                 obuf[:, b, :, MID0 - 1:MID0].to_broadcast([128, C, MID1 - MID0])).then_inc(mid_ready, 1)

        @block.scalar
        def _(act):
            def rows_evac(i):
                for gi in range(GPP):
                    act.wait_ge(rows_full, GPP * i + gi + 1)
                    act.activation(tbuf[:, gi * GI:(gi + 1) * GI, :],
                                   bank[:, gi % 4, 0:GI * NF].rearrange("p (a b) -> p a b", a=GI),
                                   ACT.Copy).then_inc(rows_out, 1)

            act.wait_ge(inv_ready, 1)
            act.activation(root[:, :], inv[:, :], ACT.Sqrt).then_inc(root_ready, 1)
            with act.Fori(0, BP) as i:
                rows_evac(i)
            with act.Fori(0, NMC // WR) as q:
                for s in range(WR):
                    act.wait_ge(mix_full, q * WR + s + 1)
                    act.activation(mixed[:, :, bass.ds((q * WR + s) * MC, MC)].rearrange("p b m -> p m b"),
                                   bank[0:C, 6 + s % 2, 0:MC * B].rearrange("p (m b) -> p m b", m=MC),
                                   ACT.Copy).then_inc(mix_out, 1)

            act.wait_ge(coef_ready, 1)
            act.wait_ge(u_static, 1)

            def u_evac(b):
                for t in range(3):
                    act.wait_ge(y_full, 3 * b + t + 1)
                    src = bank[:, 6 + t % 2, 0:JB * 2 * NEY].rearrange("p (j s e) -> p j s e", j=JB, s=2)
                    dst = u[:, E0:E1, :].rearrange("p e (s j) -> p j s e", s=2)[:, t * JB:(t + 1) * JB]
                    if t > 0:
                        for s in range(2):
                            last = act.activation(dst[:, :, s], src[:, :, s], ACT.Copy, scale=S0)
                    else:
                        for s in range(2):
                            act.activation(dst[:, 1:, s], src[:, 1:, s], ACT.Copy, scale=S0)
                        act.activation(dst[:, 0, 1], src[:, 0, 1], ACT.Copy, scale=S0)
                        for e0, e1 in ((0, EPAD - E0), (EPAD + 1 - E0, NEY)):
                            last = act.activation(dst[:, 0, 0, e0:e1], src[:, 0, 0, e0:e1], ACT.Identity,
                                                  scale=S0, bias=SH0)
                    last.then_inc(u_out, 1)
                act.wait_ge(u_out, 3 * b + 3)
                act.activation(u_hi[:, :, :], u[:, :, :], ACT.Copy).then_inc(u_hi_ready, 1)

            def z_evac(b):
                for n in range(3 * ZK):
                    k, kh = n // 3, n % 3
                    act.wait_ge(z_full, 9 * b + n + 1)
                    src = bank[:, 6 + (n + 1) % 2, 0:12 * NP].rearrange("p (e q) -> p e q", e=12)
                    dst = z[:, 12 * k:12 * k + 12, kh * NP:(kh + 1) * NP]
                    if kh == 1:
                        act.activation(dst[:, :, 0:1], src[:, :, 0:1], ACT.Identity, bias=B1)
                        last = act.activation(dst[:, :, 1:], src[:, :, 1:], ACT.Copy)
                    else:
                        last = act.activation(dst, src, ACT.Copy)
                    last.then_inc(z_out, 1)

            def zt_evac(b, g):
                act.wait_ge(zt_full, G * b + g + 1)
                if g == 4:
                    act.activation(zt[:, 1, 0:192], bank[0:3 * NP, tr_bank(False, g), 0:192], ACT.Copy)
                    act.activation(zt[:, 1, 192:320], bank[0:3 * NP, tr_bank(False, g), 192:320], ACT.Copy, scale=0.0)
                    last = act.activation(zt[:, 1, 320:512], bank[0:3 * NP, tr_bank(False, g), 320:512], ACT.Copy)
                else:
                    last = act.activation(zt[:, g % 3, :], bank[0:3 * NP, tr_bank(False, g), :], ACT.Copy)
                last.then_inc(zt_out, 1)

            def hi(b, g):
                act.wait_ge(act_ready, G * b + g + 1)
                act.activation(a_hi[:, 4 * g:4 * g + 4, 1:1 + N],
                               act_f[:, g % 3, :].rearrange("p (e h) -> p e h", e=4), ACT.Copy).then_inc(a_hi_ready, 1)

            def lift_evac(b):
                zt_evac(b, 0)
                for g in range(G):
                    if g + 1 < G:
                        zt_evac(b, g + 1)
                    act.wait_ge(z1_full, G * b + g + 1)
                    act.activation(neg[:, g % 3, :], bank[:, 3 + g % 3, :], ACT.Relu, scale=-1.0).then_inc(neg1_ready, 1)
                    if g > 0:
                        hi(b, g - 1)
                hi(b, G - 1)

            def out_evac(b, gs):
                for g in gs:
                    act.wait_ge(conv_full, G * b + g + 1)
                    act.activation(neg[:, g % 3, :], bank[:, 3 + g % 3, :], ACT.Relu, scale=-1.0).then_inc(neg2_ready, 1)

            u_evac(0)
            z_evac(0)
            with act.Fori(0, B - 1) as b:
                lift_evac(b)
                u_evac(b + 1)
                out_evac(b, range(0, 4))
                z_evac(b + 1)
                out_evac(b, range(4, G))
            lift_evac(B - 1)
            out_evac(B - 1, range(G))

        @block.vector
        def _(dve):
            steps = [0]

            def link(ins):
                steps[0] += 1
                ins.then_inc(chain, 1)
                dve.wait_ge(chain, steps[0])

            dve.memset(coef[:, 6:7], 0.0).then_inc(modes_out, 1)
            dve.memset(coef[:, 7:8], 0.0).then_inc(blur_out, 1)
            dve.memset(coef[:, 8:9], 0.0).then_inc(cols_out, G)
            dve.memset(coef[:, 9:10], 0.0).then_inc(stored, 32)

            dve.wait_ge(consts_in, 16 * NC_CONST)
            for l in range(3):
                link(dve.tensor_scalar(var[:, l:l + 1], pcol_sb[:, 4 * l + 3:4 * l + 4], EPS, None, ALU.add))
            for l in range(2):
                link(dve.tensor_scalar(var[:, 3 + l * 128:3 + (l + 1) * 128], prow_sb[:, 2 * l + 1], EPS, None, ALU.add))
            dve.reciprocal(inv[:, :], var[:, :]).then_inc(inv_ready, 1)
            dve.wait_ge(root_ready, 1)
            link(dve.tensor_tensor(inv[:, :], root[:, :], root[:, :], ALU.mult))
            link(dve.tensor_tensor(inv[:, :], inv[:, :], var[:, :], ALU.mult))
            link(dve.tensor_scalar(inv[:, :], inv[:, :], -0.5, 1.5, ALU.mult, ALU.add))
            link(dve.tensor_tensor(root[:, :], root[:, :], inv[:, :], ALU.mult))
            for l in range(3):
                g, be, m = (pcol_sb[:, 4 * l + i:4 * l + i + 1] for i in range(3))
                s = S0 if l == 0 else coef[:, 9 + l:10 + l]
                sh = (SH0, B1, B2)[l]
                link(dve.tensor_tensor(s, root[:, l:l + 1], g, ALU.mult))
                link(dve.tensor_tensor(coef[:, 13:14], m, s, ALU.mult))
                link(dve.tensor_tensor(sh, be, coef[:, 13:14], ALU.subtract))
            for l in range(2):
                link(dve.tensor_scalar((C1, C2)[l], pcol_sb[:, 12 + l:13 + l], -1.0, 1.0, ALU.mult, ALU.add))
            link(dve.memset(u[:, :, :], 0.0))
            link(dve.memset(yr[:, :, :], 0.0))
            for e0, e1 in ((0, E0), (E1, NE)):
                link(dve.tensor_scalar(u[:, e0:e1, 0], u[:, e0:e1, 0], SH0, None, ALU.add))
                link(dve.tensor_scalar(yr[:, e0:e1, 0], yr[:, e0:e1, 0], B2, None, ALU.add))
            dve.memset(coef[:, 14:15], 0.0).then_inc(coef_ready, 1)
            dve.memset(coef[:, 15:16], 0.0).then_inc(u_static, 1)
            for l in range(2):
                link(dve.tensor_tensor(prow_sb[:, 2 * l], prow_sb[:, 2 * l], root[:, 3 + l * 128:3 + (l + 1) * 128], ALU.mult))
                for t in range(6):
                    link(dve.tensor_tensor(w_f[:, l, t], w_f[:, l, t], prow_sb[:, 2 * l], ALU.mult))
                link(dve.tensor_copy(w_hi[l][:, :, :], w_f[:, l]))
                dve.tensor_tensor(w_lo[l][:, :, :], w_f[:, l], w_hi[l][:, :, :].bitcast(F32),
                                  ALU.subtract).then_inc(w_split, 1)

            def h_evac(i):
                dve.wait_ge(modes_full, i + 1)
                dve.tensor_copy(hbuf[:, i + 2, :], bank[:, 4, 0:KE * KE]).then_inc(modes_out, 1)

            def sums(t):
                dve.wait_ge(blur_full, t + 1)
                dve.tensor_copy(hblur[:, :, :], bank[:, 5, 0:KE * KE].rearrange("p (i j) -> p i j", i=KE)).then_inc(blur_out, 1)
                dve.wait_ge(blur_out, t + 2)
                v = xx[:, :, :].rearrange("p (i j) b -> p i j b", i=K)
                for s in range(2):
                    a = hblur[s * C:(s + 1) * C, 0:K, 0:K]
                    n = hblur[s * C:(s + 1) * C, K:0:-1, K:0:-1]
                    dve.tensor_tensor(v[0:C, :, :, t * 2 + s], a, n, ALU.add)
                    last = dve.tensor_tensor(v[C:2 * C, :, :, t * 2 + s], a, n, ALU.subtract)
                last.then_inc(xx_ready, 1)
                dve.wait_ge(xx_ready, t + 1)

            def edge(dsts, src, half):
                for d in dsts:
                    for s in range(2):
                        last = dve.tensor_copy(hbuf[s * C:(s + 1) * C, d, :], hbuf[half * C:(half + 1) * C, src, :])
                last.then_inc(edges, 1)

            with dve.Fori(0, 2) as i:
                h_evac(i)
            dve.wait_ge(modes_out, 2)
            edge((0, 1), 2, 0)
            with dve.Fori(2, BP) as i:
                h_evac(i)
                sums(i - 2)
            dve.wait_ge(modes_out, BP + 1)
            edge((BP + 2, BP + 3), BP + 1, 1)
            sums(BP - 2)
            sums(BP - 1)
            for n in range(8):
                g, half = n // 2, n % 2
                dve.wait_ge(turn_full, n + 1)
                dve.tensor_copy(turned[:, g, half * 8:half * 8 + 8, :],
                                bank[0:MT, n % 4, :].rearrange("p (b c) -> p b c", b=8)).then_inc(turn_out, 1)
            dve.wait_ge(modes_stored, 64)
            dve.memset(a_hi[:, :, 0:1].bitcast(F32), 0.0)
            dve.memset(a_hi[:, :, HP - 1:HP].bitcast(F32), 0.0)
            dve.memset(a_lo[:, :, 0:1].bitcast(F32), 0.0)
            dve.memset(a_lo[:, :, HP - 1:HP].bitcast(F32), 0.0)

            def yr_evac(b):
                for t in range(3):
                    dve.wait_ge(u_out, 3 * b + t + 1)
                    src = bank[:, 6 + t % 2, 0:JB * 2 * NEY].rearrange("p (j s e) -> p j s e", j=JB, s=2)
                    dst = yr[:, E0:E1, :].rearrange("p e (s j) -> p j s e", s=2)[:, t * JB:(t + 1) * JB]
                    if t > 0:
                        last = dve.tensor_copy(dst, src)
                    else:
                        dve.tensor_copy(dst[:, 1:], src[:, 1:])
                        dve.tensor_copy(dst[:, 0, 1], src[:, 0, 1])
                        last = dve.tensor_scalar(dst[:, 0, 0], src[:, 0, 0], B2, None, ALU.add)
                    last.then_inc(yr_out, 1)
                dve.wait_ge(u_hi_ready, b + 1)
                dve.tensor_tensor(u_lo[:, :, :], u[:, :, :], u_hi[:, :, :].bitcast(F32), ALU.subtract).then_inc(u_lo_ready, 1)

            def lo(b, g):
                dve.wait_ge(a_hi_ready, G * b + g + 1)
                dst = a_lo[:, 4 * g:4 * g + 4, 1:1 + N]
                last = dve.tensor_tensor(dst, act_f[:, g % 3, :].rearrange("p (e h) -> p e h", e=4),
                                         a_hi[:, 4 * g:4 * g + 4, 1:1 + N].bitcast(F32), ALU.subtract)
                if g == 0:
                    dve.tensor_copy(a_hi[:, NO, 1:1 + N], act_f[:, 0, 0:N])
                    last = dve.tensor_tensor(a_lo[:, NO, 1:1 + N], act_f[:, 0, 0:N],
                                             a_hi[:, 0, 1:1 + N].bitcast(F32), ALU.subtract)
                last.then_inc(a_lo_ready, 1)

            def lift_evac(b):
                for g in range(G):
                    dve.wait_ge(neg1_ready, G * b + g + 1)
                    if g >= 3:
                        dve.wait_ge(a_lo_ready, G * b + g - 2)
                    dve.scalar_tensor_tensor(act_f[:, g % 3, :], neg[:, g % 3, :], C1, bank[:, 3 + g % 3, :],
                                             ALU.mult, ALU.add).then_inc(act_ready, 1)
                    dve.wait_ge(yt_full, G * b + g + 1)
                    dve.tensor_copy(yt[:, g, :], bank[0:NP, tr_bank(True, g), :]).then_inc(yt_out, 1)
                    if g > 0:
                        dve.wait_ge(act_ready, G * b + g)
                        lo(b, g - 1)
                dve.wait_ge(act_ready, G * b + G)
                lo(b, G - 1)

            def out_evac(b, gs):
                for g in gs:
                    dve.wait_ge(neg2_ready, G * b + g + 1)
                    if g == 0:
                        dve.wait_ge(stored, 16 * (b + 1))
                    e = 4 * g + 1
                    runs = [(e, 4)] if g != 4 else [(e, 1), (e + 2, 2)]
                    for e0, ne in runs:
                        w0 = 2 * e0 + 92 if e0 < EPAD else 2 * (e0 - EPAD - 1)
                        q = (e0 - e) * N
                        for par in range(2):
                            rows = slice(par * C, (par + 1) * C)
                            for half in range(2):
                                cols = slice(half * 64, half * 64 + 64)
                                sneg = neg[rows, g % 3, q:q + ne * N].rearrange("p (e h) -> p e h", e=ne)[:, :, cols]
                                spos = bank[rows, 3 + g % 3, q:q + ne * N].rearrange("p (e h) -> p e h", e=ne)[:, :, cols]
                                dst = obuf[half * C:(half + 1) * C, b % 2, :, w0 + par:w0 + par + 2 * ne - 1:2]
                                last = dve.scalar_tensor_tensor(dst.rearrange("p h e -> p e h"), sneg,
                                                                C2[rows, :], spos, ALU.mult, ALU.add)
                    last.then_inc(cols_out, 1)

            yr_evac(0)
            with dve.Fori(0, B - 1) as b:
                lift_evac(b)
                yr_evac(b + 1)
                out_evac(b, range(G))
            lift_evac(B - 1)
            out_evac(B - 1, range(G))

        @block.tensor
        def _(pe):
            pe.wait_ge(consts_in, 16 * NC_CONST)

            def forward(i):
                for c in range(CPP):
                    s = c % XR
                    pe.wait_ge(x_in[s], 32 * (i * (CPP // XR) + c // XR + 1))
                    for half in range(CH // GI):
                        gi = c * (CH // GI) + half
                        if gi >= 4:
                            pe.wait_ge(rows_out, GPP * i + gi - 3)
                        for q in range(GI):
                            last = pe.matmul(bank[:, gi % 4, q * NF:(q + 1) * NF], xbuf[:, s, half * GI + q, :],
                                             fwd_sb[:, :], start=True, stop=True)
                        last.then_inc(rows_full, 1)
                pe.wait_ge(rows_out, GPP * (i + 1))
                pe.wait_ge(modes_out, i + 1)
                for e in range(KE):
                    for f in range(2):
                        last = pe.matmul(bank[:, 4, e * KE:(e + 1) * KE], tbuf[:, :, f * K + e % K],
                                         f2_sb[:, f, e, :], start=f == 0, stop=f == 1)
                last.then_inc(modes_full, 1)

            def blur(t):
                pe.wait_ge(blur_out, t + 1)
                for d in range(5):
                    last = pe.matmul(bank[:, 5, 0:KE * KE], bblur_sb[:, d, :], hbuf[:, t + d, :],
                                     start=d == 0, stop=d == 4)
                last.then_inc(blur_full, 1)

            with pe.Fori(0, 2) as i:
                forward(i)
            pe.wait_ge(edges, 1)
            with pe.Fori(2, BP) as i:
                forward(i)
                pe.wait_ge(modes_out, i + 2)
                blur(i - 2)
            pe.wait_ge(edges, 2)
            blur(BP - 2)
            blur(BP - 1)
            pe.wait_ge(xx_ready, BP)
            with pe.Fori(0, NMC // WR) as q:
                for s in range(WR):
                    pe.wait_ge(w_in[s], 16 * (q + 1))
                    if s >= 2:
                        pe.wait_ge(mix_out, q * WR + s - 1)
                    for m in range(MC):
                        last = pe.matmul(bank[0:C, 6 + s % 2, m * B:(m + 1) * B], wbuf[:, s, m, :],
                                         xx[:, (q * WR + s) * MC + m, :], start=True, stop=True)
                    last.then_inc(mix_full, 1)
                pe.wait_ge(mix_out, q * WR + WR)
            for n in range(8):
                g, half = n // 2, n % 2
                if n >= 4:
                    pe.wait_ge(turn_out, n - 3)
                for q in range(8):
                    last = pe.matmul(bank[0:MT, n % 4, q * C:(q + 1) * C],
                                     mixed[:, half * 8 + q, g * MT:(g + 1) * MT], cblur_sb[:, :], start=True, stop=True)
                last.then_inc(turn_full, 1)

            def inverse_w(b):
                pe.wait_ge(yin_in, 64 * (b + 1))
                for t in range(3):
                    if t == 2:
                        pe.wait_ge(u_out, 3 * b + 1)
                        pe.wait_ge(yr_out, 3 * b + 1)
                    for q in range(JB):
                        last = pe.matmul(bank[:, 6 + t % 2, q * 2 * NEY:(q + 1) * 2 * NEY], yin[:, t * JB + q, :],
                                         ytab_sb[:, :], start=True, stop=True)
                    last.then_inc(y_full, 1)

            def conv1(b):
                pe.wait_ge(yr_out, 3 * b + 3)
                pe.wait_ge(u_hi_ready, b + 1)
                pe.wait_ge(u_lo_ready, b + 1)
                for n in range(3 * ZK):
                    k, kh = n // 3, n % 3
                    if n >= 2:
                        pe.wait_ge(z_out, 9 * b + n - 1)
                    terms = [(w, v, t) for t in range(2) for w, v in ((w_hi[0], u_hi), (w_hi[0], u_lo), (w_lo[0], u_hi))]
                    for m, (w, v, t) in enumerate(terms):
                        last = pe.matmul(bank[:, 6 + (n + 1) % 2, 0:12 * NP], w[:, 2 * kh + t, :],
                                         v[:, 12 * k + t:12 * k + t + 12, :], start=m == 0, stop=m == len(terms) - 1)
                    last.then_inc(z_full, 1)

            def turn_z(b, g):
                if g >= 3:
                    pe.wait_ge(yt_out, G * b + g - 2)
                for q in range(4):
                    last = pe.transpose(bank[0:3 * NP, tr_bank(False, g), q * 128:(q + 1) * 128],
                                        z[:, 4 * g + q, :], ident_sb[:, :])
                last.then_inc(zt_full, 1)

            def turn_y(b, g):
                for q in range(4):
                    last = pe.transpose(bank[0:2 * NP, tr_bank(True, g), q * 128:(q + 1) * 128],
                                        yr[:, 4 * g + 1 + q:4 * g + 3 + q, :], ident_sb[:, :])
                last.then_inc(yt_full, 1)

            def lift_rows(b):
                pe.wait_ge(z_out, 9 * (b + 1))
                turn_z(b, 0)
                for g in range(G):
                    if g + 1 < G:
                        turn_z(b, g + 1)
                    pe.wait_ge(zt_out, G * b + g + 1)
                    if g < 3:
                        pe.wait_ge(cols_out, G * b + 7 + g)
                    else:
                        pe.wait_ge(act_ready, G * b + g - 2)
                    for q in range(4):
                        last = pe.matmul(bank[:, 3 + g % 3, q * N:(q + 1) * N], zt[:, g % 3, q * 128:(q + 1) * 128],
                                         lift_sb[:, :], start=True, stop=True)
                    last.then_inc(z1_full, 1)
                    if g == G - 1:
                        pe.wait_ge(yt_out, G * b + G - 2)
                    turn_y(b, g)

            def conv2(b, gs):
                for g in gs:
                    if g < 3:
                        pe.wait_ge(a_lo_ready, G * b + 7 + g)
                        pe.wait_ge(yt_out, G * b + G)
                    else:
                        pe.wait_ge(cols_out, G * b + G + g - 2)
                    m = 0
                    for t in range(2):
                        for kh in range(3):
                            for w, v in ((w_hi[1], a_hi), (w_hi[1], a_lo), (w_lo[1], a_hi)):
                                pe.matmul(bank[:, 3 + g % 3, :], w[:, 2 * kh + t, :],
                                          v[:, 4 * g + t:4 * g + t + 4, kh:kh + N], start=m == 0, stop=False)
                                m += 1
                    for q in range(4):
                        last = pe.matmul(bank[:, 3 + g % 3, q * N:(q + 1) * N], yt[:, g, q * 128:(q + 1) * 128],
                                         rowfun_sb[:, :], start=False, stop=q == 3)
                    last.then_inc(conv_full, 1)

            pe.wait_ge(w_split, 2)
            inverse_w(0)
            conv1(0)
            with pe.Fori(0, B - 1) as b:
                lift_rows(b)
                inverse_w(b + 1)
                conv2(b, range(0, 4))
                conv1(b + 1)
                conv2(b, range(4, G))
            lift_rows(B - 1)
            conv2(B - 1, range(G))


def tr_bank(is_y, g):
    if is_y:
        return (2 * g + 2 if g < G - 1 else 2 * G - 1) % 3
    return (2 * g - 1 if g else 0) % 3


def tables():
    import numpy as np

    r = np.arange(-R, R + 1, dtype=np.float32)
    kern = np.exp(-0.5 * (r / 1.0) ** 2)
    kern = (kern / kern.sum()).astype(np.float32).astype(np.float64)

    def blur_matrix(n):
        m = np.zeros((n, n))
        for i in range(n):
            for d in range(2 * R + 1):
                m[i, min(max(i + d - R, 0), n - 1)] += kern[d]
        return m

    pos = np.arange(N)
    ang = 2 * np.pi / N
    k = np.arange(K)
    ke = np.arange(KE) % K
    fwd = np.concatenate([np.cos(ang * pos[:, None] * k), np.sin(ang * pos[:, None] * k)], 1)
    cw, sw = np.cos(ang * pos[:, None] * ke), np.sin(ang * pos[:, None] * ke)
    cw1, sw1 = np.cos(ang * (pos[:, None] + 1) * ke), np.sin(ang * (pos[:, None] + 1) * ke)
    ca, sa = np.cos(ang * ke)[None, :, None], np.sin(ang * ke)[None, :, None]
    f2 = np.stack([cw[:, None] - sa * cw1[:, None] - ca * sw1[:, None],
                   -sw[:, None] - ca * cw1[:, None] + sa * sw1[:, None]], 1)
    bb = np.zeros((128, 5, 128))
    for d in range(5):
        for s in range(2):
            for t in range(2):
                tap = 2 * (d - 2) + s - t + R
                if 0 <= tap <= 2 * R:
                    bb[s * C + np.arange(C), d, t * C + np.arange(C)] = kern[tap]
    cb = blur_matrix(C).T
    blur = blur_matrix(N)
    j = np.arange(KE)
    rc, rs = blur @ np.cos(ang * pos[:, None] * j), blur @ np.sin(ang * pos[:, None] * j)
    funs = np.concatenate([rc, rs], 1).T
    lift = np.zeros((3, NP, N))
    lift[0, :, 1:] = funs[:, :-1]
    lift[1] = funs
    lift[2, :, :-1] = funs[:, 1:]
    keep = ((pos < WLO) | (pos >= WHI)).astype(np.float64)
    scale = 0.5 / (N * N)
    rc, rs = rc * keep[:, None] * scale, rs * keep[:, None] * scale
    yt = np.zeros((4 * K, 2, NEY))
    for e in range(E0, E1):
        if e == EPAD:
            continue
        for par in range(2):
            w = (2 * e + 92 if e < EPAD else 2 * (e - EPAD - 1)) + par
            at = 2 * K * par
            yt[at:at + K, 0, e - E0] = rc[w, :K]
            yt[at + K:at + 2 * K, 0, e - E0] = -rs[w, 1:]
            yt[at:at + K, 1, e - E0] = -rs[w, :K]
            yt[at + K:at + 2 * K, 1, e - E0] = -rc[w, 1:]
    out = dict(fwd=fwd, f2tab=f2, bblur=bb, cblur=cb, ytab=yt.reshape(4 * K, 2 * NEY),
               lift=lift.reshape(3 * NP, N), ident=np.eye(128))
    return {n: np.ascontiguousarray(a.astype(np.float32)) for n, a in out.items()}


def kernel(**inputs):
    import numpy as _np
    import concourse.bacc as _bacc
    from concourse import mybir as _mybir
    from concourse.bass_utils import run_bass_kernel_spmd as _run

    a = {n: _np.asarray(v) for n, v in inputs.items()}
    w0 = a["L0_conv_w1"]
    neg = (-_np.arange(K)) % K
    w0n = w0[:, :, neg][:, :, :, neg]
    wmix = _np.concatenate([w.transpose(0, 2, 3, 1).reshape(C, NM, C) for w in (w0, w0n)], 0)
    wconv = _np.zeros((2, 3, 2, 2, C, 2, C), _np.float32)
    for l, name in enumerate(("L1_conv_w1", "L1_conv_w2")):
        wt = a[name].transpose(2, 3, 1, 0)
        for t in range(2):
            for pi in range(2):
                for po in range(2):
                    kw = 2 * t + pi - po
                    if 0 <= kw <= 2:
                        wconv[l, :, t, pi, :, po, :] = wt[:, kw]
    wconv = wconv.transpose(3, 4, 0, 1, 2, 5, 6).reshape(128, 2, 6, 128)
    cols = [a[f"L1_conv_bn{l}_{p}"] for l in range(3) for p in "gbmv"] + [a["L1_conv_prelu1_a"], a["L1_conv_prelu2_a"]]
    pcol = _np.tile(_np.stack(cols, 1), (2, 1))
    rows = _np.stack([a["L1_conv_bn1_g"], a["L1_conv_bn1_v"], a["L1_conv_bn2_g"], a["L1_conv_bn2_v"]])
    prow = _np.tile(_np.tile(rows, (1, 2))[None], (128, 1, 1))

    host = dict(x=a["x"], wmix=wmix, wconv=wconv, pcol=pcol, prow=prow, **tables())
    nc = _bacc.Bacc("TRN2", target_bir_lowering=False, num_devices=1)
    arrays, args = {}, {}
    for name, v in host.items():
        v = _np.ascontiguousarray(v)
        arrays[f"in_{name}_dram"] = v
        args[name] = nc.dram_tensor(f"in_{name}_dram", v.shape, _mybir.dt.from_np(v.dtype), kind="ExternalInput").ap()
    args["out"] = nc.dram_tensor("out_0_dram", (B, C, N, N), F32, kind="ExternalOutput").ap()
    conv_seq_kernel(nc, **args)
    r = _run(nc, [arrays], core_ids=[0])
    return r.results[0]["out_0_dram"]
```

```python
from contextlib import ExitStack

import concourse.bass as bass
from concourse import mybir

ACT = mybir.ActivationFunctionType
ALU = mybir.AluOpType
F32 = mybir.dt.float32
F32R = mybir.dt.float32r

B, C, N, K = 16, 64, 128, 20
BP = B // 2
KE = K + 1
NF = 2 * K
NP = 2 * (K + 1)
NM = K * K
WLO, WHI = 33, 96
R = 4
EPS = 1e-5

CH = 16
XR = 4
CPP = 2 * C // CH
GI = 8
GPP = 2 * C // GI
MC = 25
NMC = NM // MC
WR = 8
MT = 100
WIDE, HALF = 128, 64

NE = 38
E0, E1, EPAD = 2, 36, 18
NEY = E1 - E0
NO = 36
G = 9
ZK = 3
JB = 7
HP = N + 2
MID0, MID1 = 36, 94


Z_BANK = (0, 1, 0, 1, 2, 1, 2, 0, 2)
Y_BANK = (2, 0, 1)
Y0_BANK = (6, 7, 0)


def conv_seq_kernel(nc, x, wmix, wconv, pcol, prow, fwd, f2tab, bblur, cblur, ytab, lift, rowfun, ident, out):
    xs = x.rearrange("b (n i) h w -> (b n) h i w", i=CH)
    modes = nc.dram_tensor("modes", (B, NM, C), F32, kind="Internal").ap()

    with ExitStack() as ctx:
        def sem(name):
            return ctx.enter_context(nc.semaphore(name))

        def sb(name, shape, dt=F32, stack=ctx):
            return stack.enter_context(nc.sbuf_tensor(name, shape, dt))

        bank = ctx.enter_context(nc.psum_tensor("bank", [128, 8, 512], F32))

        ident_sb = sb("ident_sb", [128, 128])
        ytab_sb = sb("ytab_sb", [4 * K, WIDE])
        lift_sb = sb("lift_sb", [3 * NP, N])
        rowfun_sb = sb("rowfun_sb", [3 * NP, 3, N])
        pcol_sb = sb("pcol_sb", [128, 14])
        coef = sb("coef", [128, 16])
        w_hi = [sb(f"w_hi{l}", [128, 6, 128], F32R) for l in range(2)]
        w_lo = [sb(f"w_lo{l}", [128, 6, 128], F32R) for l in range(2)]
        yin = sb("yin", [4 * K, KE, 128])
        u = sb("u", [128, NE, NP])
        yr = sb("yr", [128, NE, NP])
        first = ExitStack()
        bblur_sb = sb("bblur_sb", [128, 3 * 10], stack=first)
        fwd_sb = sb("fwd_sb", [128, WIDE], stack=first)
        f2_sb = sb("f2_sb", [128, 2 * KE * KE + HALF], stack=first)
        cblur_sb = sb("cblur_sb", [C, WIDE], stack=first)
        prow_sb = sb("prow_sb", [128, 4, 128], stack=first)
        w_f = sb("w_f", [128, 2, 6, 128], stack=first)
        var, inv, root = (sb(n, [128, 3 + 2 * 128], stack=first) for n in ("var", "inv", "root"))
        xbuf = sb("xbuf", [128, XR, CH, N], stack=first)
        tbuf = sb("tbuf", [128, 2 * C, NF], stack=first)
        hbuf = sb("hbuf", [128, BP + 2, KE * KE], stack=first)
        hblur = sb("hblur", [128, KE, KE], stack=first)
        xx = sb("xx", [128, NM * B + HALF - B], stack=first)
        wbuf = sb("wbuf", [128, WR, MC, C], stack=first)
        mixed = xbuf[0:C].rearrange("p r i w -> p (r i w)")[:, 0:B * NM].rearrange("p (b m) -> p b m", b=B)
        turned = tbuf[0:MT].rearrange("p i f -> p (i f)")[:, 0:4 * B * C].rearrange("p (g b c) -> p g b c", g=4, b=B)
        first.close()
        u_hi = sb("u_hi", [128, NE, NP], F32R)
        u_lo = sb("u_lo", [128, NE, NP], F32R)
        z = sb("z", [128, NO, 3 * NP])
        zt = sb("zt", [3 * NP, 3, 512])
        yt = sb("yt", [3 * NP, NO // 3, 128])
        neg = sb("neg", [128, 3, 512])
        act_f = sb("act_f", [128, 3, 512])
        a_hi = sb("a_hi", [128, NO + 1, HP], F32R)
        a_lo = sb("a_lo", [128, NO + 1, HP], F32R)
        obuf = sb("obuf", [128, 2, C, N])

        consts_in = sem("consts_in")
        fwd_in = sem("fwd_in")
        x_in = [sem(f"x_in{s}") for s in range(XR)]
        rows_full = sem("rows_full")
        rows_out = sem("rows_out")
        modes_full = sem("modes_full")
        modes_out = sem("modes_out")
        hbuf_zeroed = sem("hbuf_zeroed")
        tap_done = sem("tap_done")
        hblur_ready = sem("hblur_ready")
        xx_ready = sem("xx_ready")
        w_in = [sem(f"w_in{s}") for s in range(WR)]
        mix_full = sem("mix_full")
        mix_out = sem("mix_out")
        turn_full = sem("turn_full")
        turn_out = sem("turn_out")
        modes_stored = sem("modes_stored")
        chain = sem("chain")
        zeroed = sem("zeroed")
        w_split = sem("w_split")
        inv_ready = sem("inv_ready")
        root_ready = sem("root_ready")
        coef_ready = sem("coef_ready")
        u_static = sem("u_static")
        yin_in = sem("yin_in")
        y_full = sem("y_full")
        u_out = sem("u_out")
        yr_out = sem("yr_out")
        u_hi_ready = sem("u_hi_ready")
        u_lo_ready = sem("u_lo_ready")
        z_full = sem("z_full")
        z_out = sem("z_out")
        zt_full = sem("zt_full")
        zt_out = sem("zt_out")
        yt_full = sem("yt_full")
        yt_out = sem("yt_out")
        z1_full = sem("z1_full")
        neg1_ready = sem("neg1_ready")
        act_ready = sem("act_ready")
        a_hi_ready = sem("a_hi_ready")
        a_lo_ready = sem("a_lo_ready")
        conv_full = sem("conv_full")
        neg2_ready = sem("neg2_ready")
        cols_out = sem("cols_out")
        mid_ready = sem("mid_ready")
        stored = sem("stored")

        S0, SH0, B1, B2, C1, C2 = (coef[:, i:i + 1] for i in range(6))
        NC_CONST = 10

        block = ctx.enter_context(nc.Block())

        @block.sync
        def _(sp):
            def load_x(n, s):
                for half in range(2):
                    rows = slice(half * CH // 2, (half + 1) * CH // 2)
                    sp.dma_start(xbuf[:, s, rows], xs[n][:, rows]).then_inc(x_in[s], 16)

            sp.dma_start(fwd_sb[:, :], fwd).then_inc(fwd_in, 16)
            for s in range(XR):
                load_x(s, s)
            for dst, src in ((f2_sb[:, :], f2tab), (bblur_sb[:, :], bblur),
                             (cblur_sb[:, :], cblur), (ytab_sb[:, :], ytab), (lift_sb[:, :], lift),
                             (rowfun_sb[:, :, :], rowfun), (ident_sb[:, :], ident),
                             (pcol_sb[:, :], pcol), (prow_sb[:, :, :], prow), (w_f[:, :, :, :], wconv)):
                sp.dma_start(dst, src).then_inc(consts_in, 16)
            with sp.Fori(1, B * C // CH // XR) as r:
                for s in range(XR):
                    sp.wait_ge(rows_full, ((r - 1) * XR + s + 1) * (CH // GI))
                    load_x(r * XR + s, s)
            for g in range(4):
                sp.wait_ge(turn_out, 2 * g + 2)
                sp.dma_start(modes[:, g * MT:(g + 1) * MT, :].rearrange("b m c -> m b c"),
                             turned[:, g]).then_inc(modes_stored, 16)
            sp.wait_ge(modes_stored, 64)
            sp.wait_ge(zeroed, 1)

            def load_yin(b):
                src = modes[b].rearrange("(i j) c -> j i c", i=K)
                for q in range(4):
                    shift, par = q % 2, q // 2
                    sp.dma_start(yin[q * K:(q + 1) * K, shift:shift + K, par * C:(par + 1) * C],
                                 src).then_inc(yin_in, 16)

            def store(b, masked):
                sp.wait_ge(cols_out, G * b + 2 * G)
                sp.wait_ge(mid_ready, masked)
                sp.wait_ge(stored, 16 * b + 32)
                sp.dma_start(out[b].rearrange("c (t h) w -> t c (h w)", t=2),
                             obuf[:, b % 2].rearrange("p h w -> p (h w)")).then_inc(stored, 16)

            load_yin(0)
            sp.wait_ge(y_full, 3)
            load_yin(1)
            for b in range(2):
                sp.wait_ge(y_full, 3 * b + 6)
                load_yin(b + 2)
                store(b, b + 1)
            with sp.Fori(2, B - 2) as b:
                sp.wait_ge(y_full, 3 * b + 6)
                load_yin(b + 2)
                store(b, 2)
            store(B - 2, 2)
            store(B - 1, 2)
            sp.wait_ge(stored, 16 * (B + 2))

        @block.gpsimd
        def _(pool):
            pool.memset(yin[:, :, :], 0.0).then_inc(zeroed, 1)
            pool.wait_ge(modes_out, 4)
            for s in range(WR):
                pool.dma_start(wbuf[:, s], wmix[:, s * MC:(s + 1) * MC, :]).then_inc(w_in[s], 16)
            for s in range(WR):
                pool.wait_ge(mix_full, s + 1)
                pool.dma_start(wbuf[:, s], wmix[:, (s + WR) * MC:(s + WR + 1) * MC, :]).then_inc(w_in[s], 16)
            for b in range(2):
                pool.wait_ge(cols_out, G * (b + 2))
                pool.tensor_copy(obuf[:, b, :, MID0:MID1],
                                 obuf[:, b, :, MID0 - 1:MID0].to_broadcast([128, C, MID1 - MID0])).then_inc(mid_ready, 1)

        @block.scalar
        def _(act):
            def rows_evac(i):
                for gi in range(GPP):
                    act.wait_ge(rows_full, GPP * i + gi + 1)
                    act.activation(tbuf[:, gi * GI:(gi + 1) * GI, :],
                                   bank[:, gi % 4, 0:GI * NF].rearrange("p (a b) -> p a b", a=GI),
                                   ACT.Copy).then_inc(rows_out, 1)

            act.wait_ge(inv_ready, 1)
            act.activation(root[:, :], inv[:, :], ACT.Sqrt).then_inc(root_ready, 1)
            with act.Fori(0, BP) as i:
                rows_evac(i)
            with act.Fori(0, NMC // WR) as q:
                for s in range(WR):
                    act.wait_ge(mix_full, q * WR + s + 1)
                    act.activation(mixed[:, :, bass.ds((q * WR + s) * MC, MC)].rearrange("p b m -> p m b"),
                                   bank[0:C, 6 + s % 2, 0:MC * B].rearrange("p (m b) -> p m b", m=MC),
                                   ACT.Copy).then_inc(mix_out, 1)

            act.wait_ge(coef_ready, 1)
            act.wait_ge(u_static, 1)

            def u_evac(b):
                for t in range(3):
                    act.wait_ge(y_full, 3 * b + t + 1)
                    src = bank[:, Y0_BANK[t], 0:JB * 2 * NEY].rearrange("p (j s e) -> p j s e", j=JB, s=2)
                    dst = u[:, E0:E1, :].rearrange("p e (s j) -> p j s e", s=2)[:, t * JB:(t + 1) * JB]
                    if t > 0:
                        for s in range(2):
                            last = act.activation(dst[:, :, s], src[:, :, s], ACT.Copy, scale=S0)
                    else:
                        for s in range(2):
                            act.activation(dst[:, 1:, s], src[:, 1:, s], ACT.Copy, scale=S0)
                        act.activation(dst[:, 0, 1], src[:, 0, 1], ACT.Copy, scale=S0)
                        for e0, e1 in ((0, EPAD - E0), (EPAD + 1 - E0, NEY)):
                            last = act.activation(dst[:, 0, 0, e0:e1], src[:, 0, 0, e0:e1], ACT.Identity,
                                                  scale=S0, bias=SH0)
                    last.then_inc(u_out, 1)
                act.wait_ge(u_out, 3 * b + 3)
                act.activation(u_hi[:, :, :], u[:, :, :], ACT.Copy).then_inc(u_hi_ready, 1)

            def z_evac(b):
                for n in range(3 * ZK):
                    k, kh = n // 3, n % 3
                    act.wait_ge(z_full, 9 * b + n + 1)
                    src = bank[:, 6 + (n + 1) % 2, 0:12 * NP].rearrange("p (e q) -> p e q", e=12)
                    dst = z[:, 12 * k:12 * k + 12, kh * NP:(kh + 1) * NP]
                    if kh == 1:
                        act.activation(dst[:, :, 0:1], src[:, :, 0:1], ACT.Identity, bias=B1)
                        last = act.activation(dst[:, :, 1:], src[:, :, 1:], ACT.Copy)
                    else:
                        last = act.activation(dst, src, ACT.Copy)
                    last.then_inc(z_out, 1)

            def zt_evac(b, g):
                act.wait_ge(zt_full, G * b + g + 1)
                if g == 4:
                    act.activation(zt[:, 1, 0:192], bank[0:3 * NP, Z_BANK[g], 0:192], ACT.Copy)
                    act.activation(zt[:, 1, 192:320], bank[0:3 * NP, Z_BANK[g], 192:320], ACT.Copy, scale=0.0)
                    last = act.activation(zt[:, 1, 320:512], bank[0:3 * NP, Z_BANK[g], 320:512], ACT.Copy)
                else:
                    last = act.activation(zt[:, g % 3, :], bank[0:3 * NP, Z_BANK[g], :], ACT.Copy)
                last.then_inc(zt_out, 1)

            def hi(b, g):
                act.wait_ge(act_ready, G * b + g + 1)
                act.activation(a_hi[:, 4 * g:4 * g + 4, 1:1 + N],
                               act_f[:, g % 3, :].rearrange("p (e h) -> p e h", e=4), ACT.Copy).then_inc(a_hi_ready, 1)

            def lift_evac(b):
                zt_evac(b, 0)
                for g in range(G):
                    if g + 1 < G:
                        zt_evac(b, g + 1)
                    act.wait_ge(z1_full, G * b + g + 1)
                    act.activation(neg[:, g % 3, :], bank[:, 3 + g % 3, :], ACT.Relu, scale=-1.0).then_inc(neg1_ready, 1)
                    if g > 0:
                        hi(b, g - 1)
                hi(b, G - 1)

            def out_evac(b, gs):
                for g in gs:
                    act.wait_ge(conv_full, G * b + g + 1)
                    act.activation(neg[:, g % 3, :], bank[:, 3 + g % 3, :], ACT.Relu, scale=-1.0).then_inc(neg2_ready, 1)

            u_evac(0)
            z_evac(0)
            with act.Fori(0, B - 1) as b:
                lift_evac(b)
                u_evac(b + 1)
                out_evac(b, range(0, 4))
                z_evac(b + 1)
                out_evac(b, range(4, G))
            lift_evac(B - 1)
            out_evac(B - 1, range(G))

        @block.vector
        def _(dve):
            steps = [0]

            def link(ins):
                steps[0] += 1
                ins.then_inc(chain, 1)
                dve.wait_ge(chain, steps[0])

            dve.memset(coef[:, 6:7], 0.0).then_inc(modes_out, 1)
            dve.memset(coef[:, 8:9], 0.0).then_inc(cols_out, G)
            dve.memset(coef[:, 9:10], 0.0).then_inc(stored, 32)

            dve.wait_ge(consts_in, 16 * NC_CONST)
            for l in range(3):
                link(dve.tensor_scalar(var[:, l:l + 1], pcol_sb[:, 4 * l + 3:4 * l + 4], EPS, None, ALU.add))
            for l in range(2):
                link(dve.tensor_scalar(var[:, 3 + l * 128:3 + (l + 1) * 128], prow_sb[:, 2 * l + 1], EPS, None, ALU.add))
            dve.reciprocal(inv[:, :], var[:, :]).then_inc(inv_ready, 1)
            dve.wait_ge(root_ready, 1)
            link(dve.tensor_tensor(inv[:, :], root[:, :], root[:, :], ALU.mult))
            link(dve.tensor_tensor(inv[:, :], inv[:, :], var[:, :], ALU.mult))
            link(dve.tensor_scalar(inv[:, :], inv[:, :], -0.5, 1.5, ALU.mult, ALU.add))
            link(dve.tensor_tensor(root[:, :], root[:, :], inv[:, :], ALU.mult))
            for l in range(3):
                g, be, m = (pcol_sb[:, 4 * l + i:4 * l + i + 1] for i in range(3))
                s = S0 if l == 0 else coef[:, 9 + l:10 + l]
                sh = (SH0, B1, B2)[l]
                link(dve.tensor_tensor(s, root[:, l:l + 1], g, ALU.mult))
                link(dve.tensor_tensor(coef[:, 13:14], m, s, ALU.mult))
                link(dve.tensor_tensor(sh, be, coef[:, 13:14], ALU.subtract))
            for l in range(2):
                link(dve.tensor_scalar((C1, C2)[l], pcol_sb[:, 12 + l:13 + l], -1.0, 1.0, ALU.mult, ALU.add))
            link(dve.memset(u[:, :, :], 0.0))
            link(dve.memset(yr[:, :, :], 0.0))
            for e0, e1 in ((0, E0), (E1, NE)):
                link(dve.tensor_scalar(u[:, e0:e1, 0], u[:, e0:e1, 0], SH0, None, ALU.add))
                link(dve.tensor_scalar(yr[:, e0:e1, 0], yr[:, e0:e1, 0], B2, None, ALU.add))
            dve.memset(coef[:, 14:15], 0.0).then_inc(coef_ready, 1)
            dve.memset(coef[:, 15:16], 0.0).then_inc(u_static, 1)
            for l in range(2):
                link(dve.tensor_tensor(prow_sb[:, 2 * l], prow_sb[:, 2 * l], root[:, 3 + l * 128:3 + (l + 1) * 128], ALU.mult))
                for t in range(6):
                    link(dve.tensor_tensor(w_f[:, l, t], w_f[:, l, t], prow_sb[:, 2 * l], ALU.mult))
                link(dve.tensor_copy(w_hi[l][:, :, :], w_f[:, l]))
                dve.tensor_tensor(w_lo[l][:, :, :], w_f[:, l], w_hi[l][:, :, :].bitcast(F32),
                                  ALU.subtract).then_inc(w_split, 1)

            def taps(first, last):
                ds = [d for d in range(-2, 3) if (d >= 0 or not first) and (d <= 0 or not last)]
                return [(d, None) for d in ds] + [(d, s) for d in ds for s in range(2) if (d, s) not in ((-2, 0), (2, 1))]

            def spread(i, edge, done):
                dve.wait_ge(modes_full, i + 1)
                todo = taps(edge == 0, edge == 2)
                for n, (d, s) in enumerate(todo):
                    if s is None:
                        rows, from_rows, col = slice(0, 128), slice(0, 128), d + 2
                    else:
                        rows, from_rows, col = slice(s * C, (s + 1) * C), slice((1 - s) * C, (2 - s) * C), d + 7
                        dve.wait_ge(tap_done, done + todo.index((d, None)) + 1)
                    acc = hbuf[rows, i + d + 1, :]
                    last = dve.scalar_tensor_tensor(acc, bank[from_rows, 4, 0:KE * KE],
                                                    bblur_sb[rows, edge * 10 + col:edge * 10 + col + 1],
                                                    acc, ALU.mult, ALU.add)
                    last.then_inc(tap_done, 1)
                dve.wait_ge(tap_done, done + len(todo))
                dve.memset(coef[:, 7:8], 0.0).then_inc(modes_out, 1)

            def sums(t):
                dve.tensor_copy(hblur[:, :, :], hbuf[:, t + 1, :].rearrange("p (i j) -> p i j", i=KE)).then_inc(hblur_ready, 1)
                dve.wait_ge(hblur_ready, t + 1)
                v = xx[:, 0:NM * B].rearrange("p (i j b) -> p i j b", i=K, b=B)
                for s in range(2):
                    h = hblur[s * C:(s + 1) * C]
                    a, n = h[:, 0:K, 0:K], h[:, K:0:-1, K:0:-1]
                    dve.tensor_tensor(v[0:C, :, :, t * 2 + s], a, n, ALU.add)
                    last = dve.tensor_tensor(v[C:2 * C, :, :, t * 2 + s], a, n, ALU.subtract)
                last.then_inc(xx_ready, 1)
                dve.wait_ge(xx_ready, t + 1)

            dve.memset(xx[:, NM * B:], 0.0)
            dve.memset(hbuf[:, :, :], 0.0).then_inc(hbuf_zeroed, 1)
            dve.wait_ge(hbuf_zeroed, 1)
            n_first, n_mid = len(taps(True, False)), len(taps(False, False))
            spread(0, 0, 0)
            spread(1, 1, n_first)
            with dve.Fori(2, BP - 1) as i:
                spread(i, 1, i * n_mid + (n_first - n_mid))
                sums(i - 2)
            spread(BP - 1, 2, n_first + (BP - 2) * n_mid)
            for t in range(BP - 3, BP):
                sums(t)
            for n in range(8):
                g, half = n // 2, n % 2
                dve.wait_ge(turn_full, n + 1)
                dve.tensor_copy(turned[:, g, half * 8:half * 8 + 8, :],
                                bank[0:MT, n % 4, :].rearrange("p (b c) -> p b c", b=8)).then_inc(turn_out, 1)
            dve.wait_ge(modes_stored, 64)
            dve.memset(a_hi[:, :, 0:1].bitcast(F32), 0.0)
            dve.memset(a_hi[:, :, HP - 1:HP].bitcast(F32), 0.0)
            dve.memset(a_lo[:, :, 0:1].bitcast(F32), 0.0)
            dve.memset(a_lo[:, :, HP - 1:HP].bitcast(F32), 0.0)

            def yr_evac(b):
                for t in range(3):
                    dve.wait_ge(u_out, 3 * b + t + 1)
                    src = bank[:, Y0_BANK[t], 0:JB * 2 * NEY].rearrange("p (j s e) -> p j s e", j=JB, s=2)
                    dst = yr[:, E0:E1, :].rearrange("p e (s j) -> p j s e", s=2)[:, t * JB:(t + 1) * JB]
                    if t > 0:
                        last = dve.tensor_copy(dst, src)
                    else:
                        dve.tensor_copy(dst[:, 1:], src[:, 1:])
                        dve.tensor_copy(dst[:, 0, 1], src[:, 0, 1])
                        last = dve.tensor_scalar(dst[:, 0, 0], src[:, 0, 0], B2, None, ALU.add)
                    last.then_inc(yr_out, 1)
                dve.wait_ge(u_hi_ready, b + 1)
                dve.tensor_tensor(u_lo[:, :, :], u[:, :, :], u_hi[:, :, :].bitcast(F32), ALU.subtract).then_inc(u_lo_ready, 1)

            def lo(b, g):
                dve.wait_ge(a_hi_ready, G * b + g + 1)
                dst = a_lo[:, 4 * g:4 * g + 4, 1:1 + N]
                last = dve.tensor_tensor(dst, act_f[:, g % 3, :].rearrange("p (e h) -> p e h", e=4),
                                         a_hi[:, 4 * g:4 * g + 4, 1:1 + N].bitcast(F32), ALU.subtract)
                if g == 0:
                    dve.tensor_copy(a_hi[:, NO, 1:1 + N], act_f[:, 0, 0:N])
                    last = dve.tensor_tensor(a_lo[:, NO, 1:1 + N], act_f[:, 0, 0:N],
                                             a_hi[:, 0, 1:1 + N].bitcast(F32), ALU.subtract)
                last.then_inc(a_lo_ready, 1)

            def lift_evac(b):
                for g in range(G):
                    dve.wait_ge(neg1_ready, G * b + g + 1)
                    if g >= 3:
                        dve.wait_ge(a_lo_ready, G * b + g - 2)
                    dve.scalar_tensor_tensor(act_f[:, g % 3, :], neg[:, g % 3, :], C1, bank[:, 3 + g % 3, :],
                                             ALU.mult, ALU.add).then_inc(act_ready, 1)
                    if g % 3 == 0:
                        t = g // 3
                        dve.wait_ge(yt_full, 3 * b + t + 1)
                        dve.tensor_copy(yt[:, 4 * t:4 * t + 4, :], bank[0:3 * NP, Y_BANK[t], :].rearrange(
                            "p (q c) -> p q c", q=4)).then_inc(yt_out, 1)
                    if g > 0:
                        dve.wait_ge(act_ready, G * b + g)
                        lo(b, g - 1)
                dve.wait_ge(act_ready, G * b + G)
                lo(b, G - 1)

            def out_evac(b, gs):
                for g in gs:
                    dve.wait_ge(neg2_ready, G * b + g + 1)
                    if g == 0:
                        dve.wait_ge(stored, 16 * (b + 1))
                    e = 4 * g + 1
                    runs = [(e, 4)] if g != 4 else [(e, 1), (e + 2, 2)]
                    for e0, ne in runs:
                        w0 = 2 * e0 + 92 if e0 < EPAD else 2 * (e0 - EPAD - 1)
                        q = (e0 - e) * N
                        for par in range(2):
                            rows = slice(par * C, (par + 1) * C)
                            for half in range(2):
                                cols = slice(half * 64, half * 64 + 64)
                                sneg = neg[rows, g % 3, q:q + ne * N].rearrange("p (e h) -> p e h", e=ne)[:, :, cols]
                                spos = bank[rows, 3 + g % 3, q:q + ne * N].rearrange("p (e h) -> p e h", e=ne)[:, :, cols]
                                dst = obuf[half * C:(half + 1) * C, b % 2, :, w0 + par:w0 + par + 2 * ne - 1:2]
                                last = dve.scalar_tensor_tensor(dst.rearrange("p h e -> p e h"), sneg,
                                                                C2[rows, :], spos, ALU.mult, ALU.add)
                    last.then_inc(cols_out, 1)

            yr_evac(0)
            with dve.Fori(0, B - 1) as b:
                lift_evac(b)
                yr_evac(b + 1)
                out_evac(b, range(G))
            lift_evac(B - 1)
            out_evac(B - 1, range(G))

        @block.tensor
        def _(pe):
            pe.wait_ge(fwd_in, 16)

            def forward(i):
                for c in range(CPP):
                    s = c % XR
                    pe.wait_ge(x_in[s], 32 * (i * (CPP // XR) + c // XR + 1))
                    for half in range(CH // GI):
                        gi = c * (CH // GI) + half
                        if gi >= 4:
                            pe.wait_ge(rows_out, GPP * i + gi - 3)
                        for q in range(GI):
                            last = pe.matmul(bank[:, gi % 4, q * NF:q * NF + WIDE], xbuf[:, s, half * GI + q, :],
                                             fwd_sb[:, :], start=True, stop=True)
                        last.then_inc(rows_full, 1)
                pe.wait_ge(consts_in, 16 * NC_CONST)
                pe.wait_ge(rows_out, GPP * (i + 1))
                pe.wait_ge(modes_out, i + 1)
                for s in range(2):
                    for e in range(KE):
                        for f in range(2):
                            at = (f * KE + e) * KE
                            last = pe.matmul(bank[s * C:(s + 1) * C, 4, e * KE:e * KE + HALF],
                                             tbuf[:, s * C:(s + 1) * C, f * K + e % K],
                                             f2_sb[:, at:at + HALF], start=f == 0, stop=f == 1)
                last.then_inc(modes_full, 1)

            with pe.Fori(0, BP) as i:
                forward(i)
            pe.wait_ge(xx_ready, BP)
            with pe.Fori(0, NMC // WR) as q:
                for s in range(WR):
                    pe.wait_ge(w_in[s], 16 * (q + 1))
                    if s >= 2:
                        pe.wait_ge(mix_out, q * WR + s - 1)
                    for m in range(MC):
                        last = pe.matmul(bank[0:C, 6 + s % 2, m * B:m * B + HALF], wbuf[:, s, m, :],
                                         xx[:, bass.ds(((q * WR + s) * MC + m) * B, HALF)], start=True, stop=True)
                    last.then_inc(mix_full, 1)
                pe.wait_ge(mix_out, q * WR + WR)
            for n in range(8):
                g, half = n // 2, n % 2
                if n >= 4:
                    pe.wait_ge(turn_out, n - 3)
                for q in range(8):
                    wide = WIDE if q < 7 else C
                    last = pe.matmul(bank[0:MT, n % 4, q * C:q * C + wide],
                                     mixed[:, half * 8 + q, g * MT:(g + 1) * MT], cblur_sb[:, 0:wide],
                                     start=True, stop=True)
                last.then_inc(turn_full, 1)

            def inverse_w(b):
                pe.wait_ge(yin_in, 64 * (b + 1))
                for t in range(3):
                    for q in range(JB):
                        wide = WIDE if q < JB - 1 else 2 * NEY
                        last = pe.matmul(bank[:, Y0_BANK[t], q * 2 * NEY:q * 2 * NEY + wide],
                                         yin[:, t * JB + q, :], ytab_sb[:, 0:wide], start=True, stop=True)
                    last.then_inc(y_full, 1)

            def conv1(b):
                pe.wait_ge(yr_out, 3 * b + 3)
                pe.wait_ge(u_hi_ready, b + 1)
                pe.wait_ge(u_lo_ready, b + 1)
                for n in range(3 * ZK):
                    k, kh = n // 3, n % 3
                    if n >= 2:
                        pe.wait_ge(z_out, 9 * b + n - 1)
                    terms = [(w, v, t) for t in range(2) for w, v in ((w_hi[0], u_hi), (w_hi[0], u_lo), (w_lo[0], u_hi))]
                    for m, (w, v, t) in enumerate(terms):
                        last = pe.matmul(bank[:, 6 + (n + 1) % 2, 0:12 * NP], w[:, 2 * kh + t, :],
                                         v[:, 12 * k + t:12 * k + t + 12, :], start=m == 0, stop=m == len(terms) - 1)
                    last.then_inc(z_full, 1)

            def turn_z(b, g):
                if g in (4, 7):
                    pe.wait_ge(yt_out, 3 * b + g // 3)
                for q in range(4):
                    last = pe.transpose(bank[0:3 * NP, Z_BANK[g], q * 128:(q + 1) * 128],
                                        z[:, 4 * g + q, :], ident_sb[:, :])
                last.then_inc(zt_full, 1)

            def turn_y(t):
                for q in range(4):
                    e = E0 - 1 + 3 * (4 * t + q)
                    last = pe.transpose(bank[0:3 * NP, Y_BANK[t], q * 128:(q + 1) * 128],
                                        yr[:, e:e + 3, :], ident_sb[:, :])
                last.then_inc(yt_full, 1)

            def lift_rows(b):
                pe.wait_ge(z_out, 9 * (b + 1))
                turn_z(b, 0)
                for g in range(G):
                    if g + 1 < G:
                        turn_z(b, g + 1)
                    pe.wait_ge(zt_out, G * b + g + 1)
                    if g < 3:
                        pe.wait_ge(cols_out, G * b + 7 + g)
                    else:
                        pe.wait_ge(act_ready, G * b + g - 2)
                    for q in range(4):
                        last = pe.matmul(bank[:, 3 + g % 3, q * N:(q + 1) * N], zt[:, g % 3, q * 128:(q + 1) * 128],
                                         lift_sb[:, :], start=True, stop=True)
                    last.then_inc(z1_full, 1)
                    if g % 3 == 0:
                        turn_y(g // 3)

            def conv2(b, gs):
                for g in gs:
                    if g < 3:
                        pe.wait_ge(a_lo_ready, G * b + 7 + g)
                        pe.wait_ge(yt_out, 3 * b + 3)
                    else:
                        pe.wait_ge(cols_out, G * b + G + g - 2)
                    m = 0
                    for t in range(2):
                        for kh in range(3):
                            for w, v in ((w_hi[1], a_hi), (w_hi[1], a_lo), (w_lo[1], a_hi)):
                                pe.matmul(bank[:, 3 + g % 3, :], w[:, 2 * kh + t, :],
                                          v[:, 4 * g + t:4 * g + t + 4, kh:kh + N], start=m == 0, stop=False)
                                m += 1
                    for q in range(4):
                        n = 4 * g + q
                        last = pe.matmul(bank[:, 3 + g % 3, q * N:(q + 1) * N], yt[:, n // 3, :],
                                         rowfun_sb[:, n % 3, :], start=False, stop=q == 3)
                    last.then_inc(conv_full, 1)

            pe.wait_ge(w_split, 2)
            inverse_w(0)
            conv1(0)
            with pe.Fori(0, B - 1) as b:
                lift_rows(b)
                inverse_w(b + 1)
                conv2(b, range(0, 4))
                conv1(b + 1)
                conv2(b, range(4, G))
            lift_rows(B - 1)
            conv2(B - 1, range(G))


def tables():
    import numpy as np

    r = np.arange(-R, R + 1, dtype=np.float32)
    kern = np.exp(-0.5 * (r / 1.0) ** 2)
    kern = (kern / kern.sum()).astype(np.float32).astype(np.float64)

    def blur_matrix(n):
        m = np.zeros((n, n))
        for i in range(n):
            for d in range(2 * R + 1):
                m[i, min(max(i + d - R, 0), n - 1)] += kern[d]
        return m

    pos = np.arange(N)
    ang = 2 * np.pi / N
    k = np.arange(K)
    ke = np.arange(KE) % K
    fwd = np.concatenate([np.cos(ang * pos[:, None] * k), np.sin(ang * pos[:, None] * k)], 1)
    cw, sw = np.cos(ang * pos[:, None] * ke), np.sin(ang * pos[:, None] * ke)
    cw1, sw1 = np.cos(ang * (pos[:, None] + 1) * ke), np.sin(ang * (pos[:, None] + 1) * ke)
    ca, sa = np.cos(ang * ke)[None, :, None], np.sin(ang * ke)[None, :, None]
    f2 = np.stack([cw[:, None] - sa * cw1[:, None] - ca * sw1[:, None],
                   -sw[:, None] - ca * cw1[:, None] + sa * sw1[:, None]], 1)
    bb, mb = np.zeros((2, C, 3, 10)), blur_matrix(B)
    for edge, i in enumerate((0, 3, BP - 1)):
        for d in range(-2, 3):
            if 0 <= i + d < BP:
                for s in range(2):
                    bb[s, :, edge, d + 2] = mb[2 * (i + d) + s, 2 * i + s]
                    bb[s, :, edge, d + 7] = mb[2 * (i + d) + s, 2 * i + 1 - s]
    bb = bb.reshape(128, 30)
    cb = blur_matrix(C).T
    blur = blur_matrix(N)
    j = np.arange(KE)
    rc, rs = blur @ np.cos(ang * pos[:, None] * j), blur @ np.sin(ang * pos[:, None] * j)
    funs = np.concatenate([rc, rs], 1).T
    lift = np.zeros((3, NP, N))
    lift[0, :, 1:] = funs[:, :-1]
    lift[1] = funs
    lift[2, :, :-1] = funs[:, 1:]
    rowfun = np.zeros((3, NP, 3, N))
    for q in range(3):
        rowfun[q, :, q] = funs
    rowfun = rowfun.reshape(3 * NP, 3, N)
    keep = ((pos < WLO) | (pos >= WHI)).astype(np.float64)
    scale = 0.5 / (N * N)
    rc, rs = rc * keep[:, None] * scale, rs * keep[:, None] * scale
    yt = np.zeros((4 * K, 2, NEY))
    for e in range(E0, E1):
        if e == EPAD:
            continue
        for par in range(2):
            w = (2 * e + 92 if e < EPAD else 2 * (e - EPAD - 1)) + par
            at = 2 * K * par
            yt[at:at + K, 0, e - E0] = rc[w, :K]
            yt[at + K:at + 2 * K, 0, e - E0] = -rs[w, 1:]
            yt[at:at + K, 1, e - E0] = -rs[w, :K]
            yt[at + K:at + 2 * K, 1, e - E0] = -rc[w, 1:]
    fwd = np.pad(fwd, ((0, 0), (0, WIDE - NF)))
    f2 = np.pad(f2.reshape(N, 2 * KE * KE), ((0, 0), (0, HALF)))
    cb = np.pad(cb, ((0, 0), (0, WIDE - C)))
    out = dict(fwd=fwd, f2tab=f2, bblur=bb, cblur=cb, ytab=np.pad(yt.reshape(4 * K, 2 * NEY), ((0, 0), (0, WIDE - 2 * NEY))),
               lift=lift.reshape(3 * NP, N), rowfun=rowfun, ident=np.eye(128))
    return {n: np.ascontiguousarray(a.astype(np.float32)) for n, a in out.items()}


def kernel(**inputs):
    import numpy as _np
    import concourse.bacc as _bacc
    from concourse import mybir as _mybir
    from concourse.bass_utils import run_bass_kernel_spmd as _run

    a = {n: _np.asarray(v) for n, v in inputs.items()}
    w0 = a["L0_conv_w1"]
    neg = (-_np.arange(K)) % K
    w0n = w0[:, :, neg][:, :, :, neg]
    wmix = _np.concatenate([w.transpose(0, 2, 3, 1).reshape(C, NM, C) for w in (w0, w0n)], 0)
    wconv = _np.zeros((2, 3, 2, 2, C, 2, C), _np.float32)
    for l, name in enumerate(("L1_conv_w1", "L1_conv_w2")):
        wt = a[name].transpose(2, 3, 1, 0)
        for t in range(2):
            for pi in range(2):
                for po in range(2):
                    kw = 2 * t + pi - po
                    if 0 <= kw <= 2:
                        wconv[l, :, t, pi, :, po, :] = wt[:, kw]
    wconv = wconv.transpose(3, 4, 0, 1, 2, 5, 6).reshape(128, 2, 6, 128)
    cols = [a[f"L1_conv_bn{l}_{p}"] for l in range(3) for p in "gbmv"] + [a["L1_conv_prelu1_a"], a["L1_conv_prelu2_a"]]
    pcol = _np.tile(_np.stack(cols, 1), (2, 1))
    rows = _np.stack([a["L1_conv_bn1_g"], a["L1_conv_bn1_v"], a["L1_conv_bn2_g"], a["L1_conv_bn2_v"]])
    prow = _np.tile(_np.tile(rows, (1, 2))[None], (128, 1, 1))

    host = dict(x=a["x"], wmix=wmix, wconv=wconv, pcol=pcol, prow=prow, **tables())
    nc = _bacc.Bacc("TRN2", target_bir_lowering=False, num_devices=1)
    arrays, args = {}, {}
    for name, v in host.items():
        v = _np.ascontiguousarray(v)
        arrays[f"in_{name}_dram"] = v
        args[name] = nc.dram_tensor(f"in_{name}_dram", v.shape, _mybir.dt.from_np(v.dtype), kind="ExternalInput").ap()
    args["out"] = nc.dram_tensor("out_0_dram", (B, C, N, N), F32, kind="ExternalOutput").ap()
    conv_seq_kernel(nc, **args)
    r = _run(nc, [arrays], core_ids=[0])
    return r.results[0]["out_0_dram"]
```

```python
from contextlib import ExitStack

import concourse.bass as bass
from concourse import mybir

ACT = mybir.ActivationFunctionType
ALU = mybir.AluOpType
F32 = mybir.dt.float32
F32R = mybir.dt.float32r

B, C, N, K = 16, 64, 128, 20
BP = B // 2
KE = K + 1
NF = 2 * K
NP = 2 * (K + 1)
NM = K * K
WLO, WHI = 33, 96
R = 4
EPS = 1e-5

CH = 16
XR = 4
CPP = 2 * C // CH
GI = 8
GPP = 2 * C // GI
MC = 25
NMC = NM // MC
WR = 8
MT = 100
PARTS = ((0, 4), (4, 8), (8, 16))
TURNS = [(p, g) for p in range(len(PARTS)) for g in range(4)]
WIDE, HALF = 128, 64

NE = 38
E0, E1, EPAD = 2, 36, 18
NEY = E1 - E0
NO = 36
G = 9
ZK = 3
JB = 7
HP = N + 2
MID0, MID1 = 36, 94

LA = 3
A_BANK, B_BANK, Z1_BANK, TURN_BANK = (0, 1, 2), 3, 4, 5
Y0_BANK, Z_BANK, Y_BANK = (7, 6, 7), (6, 7, 6, 6, 7, 6, 6, 6, 7), (7, 7, 6)
Z_PREV = (0, 0, 1, 3, 2, 4, 6, 7)
INVERSE_AT = {0: (0, 1), 1: (2,)}
YT_REST_AT = {1: 1, 5: 2}
U_SPLIT_AT = 2
CONV1_AT = {3: (0, 1), 4: (2,), 5: (3,), 6: (4, 5), 7: (6,), 8: (7, 8)}
TURN_Y_AT = {7: 0, 8: 1, 0: 2}
VS = 12
FILL = 8


def conv_seq_kernel(nc, x, wmix, wconv, pcol, prow, fwd, f2tab, bblur, cblur, ytab, lift, rowfun, ident, out):
    xs = x.rearrange("b (n i) h w -> (b n) h i w", i=CH)
    modes = nc.dram_tensor("modes", (B, NM, C), F32, kind="Internal").ap()

    with ExitStack() as ctx:
        def sem(name):
            return ctx.enter_context(nc.semaphore(name))

        def sb(name, shape, dt=F32, stack=ctx):
            return stack.enter_context(nc.sbuf_tensor(name, shape, dt))

        bank = ctx.enter_context(nc.psum_tensor("bank", [128, 8, 512], F32))

        ident_sb = sb("ident_sb", [128, 128])
        ytab_sb = sb("ytab_sb", [4 * K, WIDE])
        lift_sb = sb("lift_sb", [3 * NP, N])
        rowfun_sb = sb("rowfun_sb", [3 * NP, 3, N])
        rowfun_hi = sb("rowfun_hi", [3 * NP, 3, N], F32R)
        rowfun_lo = sb("rowfun_lo", [3 * NP, 3, N], F32R)
        pcol_sb = sb("pcol_sb", [128, 14])
        coef = sb("coef", [128, 18])
        w_hi = [sb(f"w_hi{l}", [128, (6, 8)[l], 128], F32R) for l in range(2)]
        w_lo = [sb(f"w_lo{l}", [128, (6, 8)[l], 128], F32R) for l in range(2)]
        yin = sb("yin", [4 * K, KE, 128])
        u = sb("u", [128, NE, NP])
        yr = sb("yr", [128, NE, NP])
        first = ExitStack()
        bblur_sb = sb("bblur_sb", [128, 3 * 10], stack=first)
        fwd_sb = sb("fwd_sb", [128, WIDE], stack=first)
        f2_sb = sb("f2_sb", [128, 2 * KE * KE + HALF], stack=first)
        cblur_sb = sb("cblur_sb", [C, WIDE], stack=first)
        prow_sb = sb("prow_sb", [128, 4, 128], stack=first)
        w_f = sb("w_f", [128, 2, 6, 128], stack=first)
        var, inv, root = (sb(n, [128, 3 + 2 * 128], stack=first) for n in ("var", "inv", "root"))
        xbuf = sb("xbuf", [128, XR, CH, N], stack=first)
        tbuf = sb("tbuf", [128, 2 * C, NF], stack=first)
        hbuf = sb("hbuf", [128, BP + 2, KE * KE], stack=first)
        hblur = sb("hblur", [128, KE, KE], stack=first)
        xx = sb("xx", [128, NM * B + HALF - B], stack=first)
        w_g = xx[:, 0:8 * 128].rearrange("p (n c) -> p n c", n=8)
        wbuf = sb("wbuf", [128, WR, MC, C], stack=first)
        mixed = xbuf[0:C].rearrange("p r i w -> p (r i w)")[:, 0:B * NM].rearrange("p (b m) -> p b m", b=B)
        turned = tbuf[0:MT].rearrange("p i f -> p (i f)")[:, 0:4 * B * C].rearrange("p (g b c) -> p g b c", g=4, b=B)
        first.close()
        u_hi = sb("u_hi", [128, NE, NP], F32R)
        u_lo = sb("u_lo", [128, NE, NP], F32R)
        z = sb("z", [128, NO, 3 * NP])
        zt = sb("zt", [3 * NP, 512])
        yt = sb("yt", [3 * NP, NO // 3, 128])
        yt_hi = sb("yt_hi", [3 * NP, NO // 3, 128], F32R)
        yt_lo = sb("yt_lo", [3 * NP, NO // 3, 128], F32R)
        neg1 = sb("neg1", [128, 512])
        act_f = sb("act_f", [128, 4, HP])
        v_f = sb("v_f", [128, 4, 4, N // 2])
        v_hi = sb("v_hi", [128, VS + 2, 4, N // 2], F32R)
        v_lo = sb("v_lo", [128, VS + 2, 4, N // 2], F32R)
        m12 = sb("m12", [128, 4, 2, N // 2])
        pq = sb("pq", [128, 4, 2, N // 2])
        y2 = sb("y2", [128, 512])
        neg2 = sb("neg2", [128, 512])
        obuf = sb("obuf", [128, 2, C, N])

        consts_in = sem("consts_in")
        fwd_in = sem("fwd_in")
        x_in = [sem(f"x_in{s}") for s in range(XR)]
        rows_full = sem("rows_full")
        rows_out = sem("rows_out")
        modes_full = sem("modes_full")
        modes_out = sem("modes_out")
        hbuf_zeroed = sem("hbuf_zeroed")
        tap_done = sem("tap_done")
        hblur_ready = sem("hblur_ready")
        xx_ready = sem("xx_ready")
        w_in = [sem(f"w_in{s}") for s in range(WR)]
        mix_full = sem("mix_full")
        mix_out = sem("mix_out")
        turn_full = sem("turn_full")
        turn_out = sem("turn_out")
        modes_stored = [sem(f"modes_stored{p}") for p in range(len(PARTS))]
        chain = sem("chain")
        zeroed = sem("zeroed")
        w_split = sem("w_split")
        inv_ready = sem("inv_ready")
        root_ready = sem("root_ready")
        coef_ready = sem("coef_ready")
        u_static = sem("u_static")
        yin_in = sem("yin_in")
        y_full = sem("y_full")
        u_out = sem("u_out")
        yr_out = sem("yr_out")
        u_hi_ready = sem("u_hi_ready")
        u_lo_ready = sem("u_lo_ready")
        z_full = sem("z_full")
        z_out = sem("z_out")
        zt_full = sem("zt_full")
        zt_out = sem("zt_out")
        yt_full = sem("yt_full")
        yt_out = sem("yt_out")
        yt_hi_ready = sem("yt_hi_ready")
        yt_lo_ready = sem("yt_lo_ready")
        z1_full = sem("z1_full")
        neg1_ready = sem("neg1_ready")
        act_ready = sem("act_ready")
        v_ready = sem("v_ready")
        v1_ready = sem("v1_ready")
        v_hi_ready = sem("v_hi_ready")
        v_lo_ready = sem("v_lo_ready")
        kept = sem("kept")
        wrapped = sem("wrapped")
        m12_full = sem("m12_full")
        m12_out = sem("m12_out")
        pq_ready = sem("pq_ready")
        conv_full = sem("conv_full")
        y2_ready = sem("y2_ready")
        act_zeroed = sem("act_zeroed")
        neg2_ready = sem("neg2_ready")
        cols_out = sem("cols_out")
        mid_ready = sem("mid_ready")
        stored = sem("stored")

        S0, SH0, B1, B2, C1, C2 = (coef[:, i:i + 1] for i in range(6))
        NC_CONST = 10

        block = ctx.enter_context(nc.Block())

        @block.sync
        def _(sp):
            def load_x(n, s):
                for half in range(2):
                    rows = slice(half * CH // 2, (half + 1) * CH // 2)
                    sp.dma_start(xbuf[:, s, rows], xs[n][:, rows]).then_inc(x_in[s], 16)

            sp.dma_start(fwd_sb[:, :], fwd).then_inc(fwd_in, 16)
            for s in range(XR):
                load_x(s, s)
            def reload_x(r):
                for s in range(XR):
                    sp.wait_ge(rows_full, ((r - 1) * XR + s + 1) * (CH // GI))
                    load_x(r * XR + s, s)

            reload_x(1)
            for dst, src in ((f2_sb[:, :], f2tab), (bblur_sb[:, :], bblur),
                             (cblur_sb[:, :], cblur), (ytab_sb[:, :], ytab), (lift_sb[:, :], lift),
                             (rowfun_sb[:, :, :], rowfun), (ident_sb[:, :], ident),
                             (pcol_sb[:, :], pcol), (prow_sb[:, :, :], prow), (w_f[:, :, :, :], wconv)):
                sp.dma_start(dst, src).then_inc(consts_in, 16)
            with sp.Fori(2, B * C // CH // XR) as r:
                reload_x(r)

            def load_yin(b):
                src = modes[b].rearrange("(i j) c -> j i c", i=K)
                for q in range(4):
                    shift, par = q % 2, q // 2
                    sp.dma_start(yin[q * K:(q + 1) * K, shift:shift + K, par * C:(par + 1) * C],
                                 src).then_inc(yin_in, 16)

            def store(b, masked):
                sp.wait_ge(cols_out, G * b + 2 * G)
                sp.wait_ge(mid_ready, masked)
                sp.wait_ge(stored, 16 * b + 32)
                sp.dma_start(out[b].rearrange("c (t h) w -> t c (h w)", t=2),
                             obuf[:, b % 2].rearrange("p h w -> p (h w)")).then_inc(stored, 16)

            for n, (p, g) in enumerate(TURNS):
                b0, b1 = PARTS[p]
                sp.wait_ge(turn_out, n + 1)
                sp.dma_start(modes[b0:b1, g * MT:(g + 1) * MT, :].rearrange("b m c -> m b c"),
                             turned[:, g, b0:b1]).then_inc(modes_stored[p], 16)
                if n == 3:
                    sp.wait_ge(zeroed, 1)
                    sp.wait_ge(modes_stored[0], 64)
                    load_yin(0)
            for p in range(1, len(PARTS)):
                sp.wait_ge(modes_stored[p], 64)
            sp.wait_ge(y_full, 3)
            load_yin(1)
            for b in range(2):
                sp.wait_ge(y_full, 3 * b + 6)
                load_yin(b + 2)
                store(b, FILL * (b + 1))
            with sp.Fori(2, B - 2) as b:
                sp.wait_ge(y_full, 3 * b + 6)
                load_yin(b + 2)
                store(b, 2 * FILL)
            store(B - 2, 2 * FILL)
            def store_last(cols):
                for t in range(2):
                    sp.dma_start(out[B - 1][:, t * C:(t + 1) * C, cols],
                                 obuf[t * C:(t + 1) * C, (B - 1) % 2, :, cols]).then_inc(stored, 16)

            sp.wait_ge(cols_out, G * B + 5)
            sp.wait_ge(stored, 16 * (B + 1))
            store_last(slice(MID0, N))
            sp.wait_ge(cols_out, G * B + G)
            sp.wait_ge(stored, 16 * (B + 3))
            store_last(slice(0, MID0))
            sp.wait_ge(stored, 16 * (B + 5))

        @block.gpsimd
        def _(pool):
            pool.memset(yin[:, :, :], 0.0).then_inc(zeroed, 1)
            for s in range(WR):
                if s % 2 == 0:
                    pool.wait_ge(modes_out, 2 + s // 2)
                pool.dma_start(wbuf[:, s], wmix[:, s * MC:(s + 1) * MC, :]).then_inc(w_in[s], 16)
            for s in range(WR):
                pool.wait_ge(mix_full, s + 1)
                pool.dma_start(wbuf[:, s], wmix[:, (s + WR) * MC:(s + WR + 1) * MC, :]).then_inc(w_in[s], 16)

            def transform(j):
                pool.wait_ge(act_ready, j + 1)
                pool.tensor_tensor(v_f[:, :, 0:4:3, :], act_f[:, :, 0:N].rearrange("p e (h s) -> p e s h", s=2),
                                   act_f[:, :, 2:2 + N].rearrange("p e (h s) -> p e s h", s=2), ALU.subtract)
                pool.tensor_tensor(v_f[:, :, 2, :], act_f[:, :, 2:2 + N:2], act_f[:, :, 1:1 + N:2],
                                   ALU.subtract).then_inc(v_ready, 1)

            def sums_and_differences(g):
                pool.wait_ge(m12_out, g + 2)
                pool.wait_ge(y2_ready, g + 3)
                pool.tensor_tensor(pq[:, :, 0], m12[:, :, 0], m12[:, :, 1], ALU.add)
                pool.tensor_tensor(pq[:, :, 1], m12[:, :, 0], m12[:, :, 1], ALU.subtract).then_inc(pq_ready, 1)

            def work(j):
                sums_and_differences(j - LA)
                transform(j)

            ahead = G + LA
            for j in range(LA):
                transform(j)
            with pool.Fori(LA, ahead) as j:
                work(j)
            for b in range(2):
                pool.wait_ge(cols_out, G * (b + 2))
                for f in range(FILL):
                    rows = slice(f * C // FILL, (f + 1) * C // FILL)
                    pool.tensor_copy(obuf[:, b, rows, MID0:MID1],
                                     obuf[:, b, rows, MID0 - 1:MID0].to_broadcast([128, C // FILL, MID1 - MID0])).then_inc(mid_ready, 1)
                    if b == 0:
                        work(ahead + f)
                if b == 0:
                    work(ahead + FILL)
            with pool.Fori(ahead + G, B * G) as j:
                work(j)
            for g in range(B * G - LA, B * G):
                sums_and_differences(g)

        @block.scalar
        def _(act):
            def rows_evac(i):
                for gi in range(GPP):
                    act.wait_ge(rows_full, GPP * i + gi + 1)
                    act.activation(tbuf[:, gi * GI:(gi + 1) * GI, :],
                                   bank[:, gi % 4, 0:GI * NF].rearrange("p (a b) -> p a b", a=GI),
                                   ACT.Copy).then_inc(rows_out, 1)

            rows_evac(0)
            act.wait_ge(inv_ready, 1)
            act.activation(root[:, :], inv[:, :], ACT.Sqrt).then_inc(root_ready, 1)
            with act.Fori(1, BP) as i:
                rows_evac(i)
            with act.Fori(0, NMC // WR) as q:
                for s in range(WR):
                    act.wait_ge(mix_full, q * WR + s + 1)
                    act.activation(mixed[:, :, bass.ds((q * WR + s) * MC, MC)].rearrange("p b m -> p m b"),
                                   bank[0:C, 6 + s % 2, 0:MC * B].rearrange("p (m b) -> p m b", m=MC),
                                   ACT.Copy).then_inc(mix_out, 1)

            act.wait_ge(coef_ready, 1)
            act.wait_ge(u_static, 1)

            def u_evac(b, ts):
                for t in ts:
                    act.wait_ge(y_full, 3 * b + t + 1)
                    src = bank[:, Y0_BANK[t], 0:JB * 2 * NEY].rearrange("p (j s e) -> p j s e", j=JB, s=2)
                    dst = u[:, E0:E1, :].rearrange("p e (s j) -> p j s e", s=2)[:, t * JB:(t + 1) * JB]
                    if t > 0:
                        for s in range(2):
                            last = act.activation(dst[:, :, s], src[:, :, s], ACT.Copy, scale=S0)
                    else:
                        for s in range(2):
                            act.activation(dst[:, 1:, s], src[:, 1:, s], ACT.Copy, scale=S0)
                        act.activation(dst[:, 0, 1], src[:, 0, 1], ACT.Copy, scale=S0)
                        for e0, e1 in ((0, EPAD - E0), (EPAD + 1 - E0, NEY)):
                            last = act.activation(dst[:, 0, 0, e0:e1], src[:, 0, 0, e0:e1], ACT.Identity,
                                                  scale=S0, bias=SH0)
                    last.then_inc(u_out, 1)

            def u_split(b):
                act.wait_ge(u_out, 3 * b + 3)
                act.activation(u_hi[:, :, :], u[:, :, :], ACT.Copy).then_inc(u_hi_ready, 1)

            def z_evac(b, ns):
                for n in ns:
                    k, kh = n // 3, n % 3
                    act.wait_ge(z_full, 9 * b + n + 1)
                    src = bank[:, Z_BANK[n], 0:12 * NP].rearrange("p (e q) -> p e q", e=12)
                    dst = z[:, 12 * k:12 * k + 12, kh * NP:(kh + 1) * NP]
                    if kh == 1:
                        act.activation(dst[:, :, 0:1], src[:, :, 0:1], ACT.Identity, bias=B1)
                        last = act.activation(dst[:, :, 1:], src[:, :, 1:], ACT.Copy)
                    else:
                        last = act.activation(dst, src, ACT.Copy)
                    last.then_inc(z_out, 1)

            def zt_evac(b, j):
                act.wait_ge(zt_full, G * b + j + 1)
                if j % G == 4:
                    act.activation(zt[:, 0:192], bank[0:3 * NP, TURN_BANK, 0:192], ACT.Copy)
                    act.activation(zt[:, 192:320], bank[0:3 * NP, TURN_BANK, 192:320], ACT.Copy, scale=0.0)
                    last = act.activation(zt[:, 320:512], bank[0:3 * NP, TURN_BANK, 320:512], ACT.Copy)
                else:
                    last = act.activation(zt[:, :], bank[0:3 * NP, TURN_BANK, :], ACT.Copy)
                last.then_inc(zt_out, 1)

            def yt_split(b, t):
                act.wait_ge(yt_out, 3 * b + t + 1)
                act.activation(yt_hi[:, 4 * t:4 * t + 4, :], yt[:, 4 * t:4 * t + 4, :], ACT.Copy).then_inc(yt_hi_ready, 1)

            def neg_lift(b, j):
                act.wait_ge(z1_full, G * b + j + 1)
                act.activation(neg1[:, :], bank[:, Z1_BANK, :], ACT.Relu, scale=-1.0).then_inc(neg1_ready, 1)

            def hi(b, j):
                act.wait_ge(v_ready, G * b + j + 1)
                act.wait_ge(v1_ready, G * b + j + 1)
                at = 4 * (j % 3)
                last = act.activation(v_hi[:, at:at + 4], v_f[:, :, :, :], ACT.Copy)
                if j % 3 == 0:
                    last = act.activation(v_hi[:, VS], v_f[:, 0], ACT.Copy)
                last.then_inc(v_hi_ready, 1)

            def step(b, g, more):
                if 0 <= g + LA - 1 < more:
                    hi(b, g + LA - 1)
                if g >= 0:
                    act.wait_ge(m12_full, G * b + g + 1)
                    act.activation(m12[:, :, :, :], bank[:, B_BANK, :].rearrange("p (e s h) -> p e s h", e=4, s=2),
                                   ACT.Copy).then_inc(m12_out, 1)
                if g + LA < more:
                    neg_lift(b, g + LA)
                if g + LA + 1 < more:
                    zt_evac(b, g + LA + 1)
                if g == U_SPLIT_AT and more > G:
                    u_split(b + 1)
                if g >= 0:
                    act.wait_ge(y2_ready, G * b + g + 4)
                    act.activation(neg2[:, :], y2[:, :], ACT.Relu, scale=-1.0).then_inc(neg2_ready, 1)
                if g == 0:
                    yt_split(b, TURN_Y_AT[0])
                elif g in TURN_Y_AT and more > G:
                    yt_split(b + 1, TURN_Y_AT[g])

            u_evac(0, range(3))
            for p in range(len(PARTS)):
                act.wait_ge(modes_stored[p], 64)
            u_split(0)
            z_evac(0, range(9))
            yt_split(0, 0)
            yt_split(0, 1)
            zt_evac(0, 0)
            for g in range(-LA, 0):
                step(0, g, 2 * G)
            with act.Fori(0, B - 1) as b:
                for g in range(G):
                    step(b, g, 2 * G)
                    u_evac(b + 1, INVERSE_AT.get(g, ()))
                    z_evac(b + 1, CONV1_AT.get(g, ()))
            for g in range(G):
                step(B - 1, g, G)

        @block.vector
        def _(dve):
            steps = [0]

            def link(ins):
                steps[0] += 1
                ins.then_inc(chain, 1)
                dve.wait_ge(chain, steps[0])

            dve.memset(coef[:, 16:17], 0.0).then_inc(m12_out, 1)
            dve.memset(coef[:, 17:18], 0.0).then_inc(y2_ready, 3)
            dve.memset(coef[:, 6:7], 0.0).then_inc(modes_out, 1)
            dve.memset(coef[:, 8:9], 0.0).then_inc(cols_out, G)
            dve.memset(coef[:, 9:10], 0.0).then_inc(stored, 32)

            dve.wait_ge(consts_in, 16 * NC_CONST)
            for l in range(3):
                link(dve.tensor_scalar(var[:, l:l + 1], pcol_sb[:, 4 * l + 3:4 * l + 4], EPS, None, ALU.add))
            for l in range(2):
                link(dve.tensor_scalar(var[:, 3 + l * 128:3 + (l + 1) * 128], prow_sb[:, 2 * l + 1], EPS, None, ALU.add))
            dve.reciprocal(inv[:, :], var[:, :]).then_inc(inv_ready, 1)
            dve.wait_ge(root_ready, 1)
            link(dve.tensor_tensor(inv[:, :], root[:, :], root[:, :], ALU.mult))
            link(dve.tensor_tensor(inv[:, :], inv[:, :], var[:, :], ALU.mult))
            link(dve.tensor_scalar(inv[:, :], inv[:, :], -0.5, 1.5, ALU.mult, ALU.add))
            link(dve.tensor_tensor(root[:, :], root[:, :], inv[:, :], ALU.mult))
            for l in range(3):
                g, be, m = (pcol_sb[:, 4 * l + i:4 * l + i + 1] for i in range(3))
                s = S0 if l == 0 else coef[:, 9 + l:10 + l]
                sh = (SH0, B1, B2)[l]
                link(dve.tensor_tensor(s, root[:, l:l + 1], g, ALU.mult))
                link(dve.tensor_tensor(coef[:, 13:14], m, s, ALU.mult))
                link(dve.tensor_tensor(sh, be, coef[:, 13:14], ALU.subtract))
            for l in range(2):
                link(dve.tensor_scalar((C1, C2)[l], pcol_sb[:, 12 + l:13 + l], -1.0, 1.0, ALU.mult, ALU.add))
            link(dve.memset(u[:, :, :], 0.0))
            link(dve.memset(yr[:, :, :], 0.0))
            for e0, e1 in ((0, E0), (E1, NE)):
                link(dve.tensor_scalar(u[:, e0:e1, 0], u[:, e0:e1, 0], SH0, None, ALU.add))
                link(dve.tensor_scalar(yr[:, e0:e1, 0], yr[:, e0:e1, 0], B2, None, ALU.add))
            dve.memset(coef[:, 14:15], 0.0).then_inc(coef_ready, 1)
            dve.memset(coef[:, 15:16], 0.0).then_inc(u_static, 1)
            link(dve.tensor_copy(rowfun_hi[:, :, :], rowfun_sb[:, :, :]))
            link(dve.tensor_tensor(rowfun_lo[:, :, :], rowfun_sb[:, :, :], rowfun_hi[:, :, :].bitcast(F32), ALU.subtract))
            for l in range(2):
                link(dve.tensor_tensor(prow_sb[:, 2 * l], prow_sb[:, 2 * l], root[:, 3 + l * 128:3 + (l + 1) * 128], ALU.mult))
                for t in range(6):
                    link(dve.tensor_tensor(w_f[:, l, t], w_f[:, l, t], prow_sb[:, 2 * l], ALU.mult))
                src = w_f[:, 0]
                if l == 1:
                    src, g = w_g[:, :, :], [w_f[:, 1, 2 * k:2 * k + 2] for k in range(3)]
                    link(dve.tensor_tensor(w_g[:, 6:8], g[0], g[2], ALU.add))
                    link(dve.tensor_tensor(w_g[:, 2:4], w_g[:, 6:8], g[1], ALU.add))
                    link(dve.tensor_tensor(w_g[:, 4:6], w_g[:, 6:8], g[1], ALU.subtract))
                    link(dve.tensor_scalar(w_g[:, 2:6], w_g[:, 2:6], 0.5, None, ALU.mult))
                    link(dve.tensor_copy(w_g[:, 0:2], g[0]))
                    link(dve.tensor_scalar(w_g[:, 6:8], g[2], -1.0, None, ALU.mult))
                link(dve.tensor_copy(w_hi[l][:, :, :], src))
                dve.tensor_tensor(w_lo[l][:, :, :], src, w_hi[l][:, :, :].bitcast(F32),
                                  ALU.subtract).then_inc(w_split, 1)

            dve.wait_ge(w_split, 2)

            def taps(first, last):
                ds = [d for d in range(-2, 3) if (d >= 0 or not first) and (d <= 0 or not last)]
                return [(d, None) for d in ds] + [(d, s) for d in ds for s in range(2) if (d, s) not in ((-2, 0), (2, 1))]

            def spread(i, edge, done):
                dve.wait_ge(modes_full, i + 1)
                todo = taps(edge == 0, edge == 2)
                for n, (d, s) in enumerate(todo):
                    if s is None:
                        rows, from_rows, col = slice(0, 128), slice(0, 128), d + 2
                    else:
                        rows, from_rows, col = slice(s * C, (s + 1) * C), slice((1 - s) * C, (2 - s) * C), d + 7
                        dve.wait_ge(tap_done, done + todo.index((d, None)) + 1)
                    acc = hbuf[rows, i + d + 1, :]
                    last = dve.scalar_tensor_tensor(acc, bank[from_rows, 4, 0:KE * KE],
                                                    bblur_sb[rows, edge * 10 + col:edge * 10 + col + 1],
                                                    acc, ALU.mult, ALU.add)
                    last.then_inc(tap_done, 1)
                dve.wait_ge(tap_done, done + len(todo))
                dve.memset(coef[:, 7:8], 0.0).then_inc(modes_out, 1)

            def sums(t):
                dve.tensor_copy(hblur[:, :, :], hbuf[:, t + 1, :].rearrange("p (i j) -> p i j", i=KE)).then_inc(hblur_ready, 1)
                dve.wait_ge(hblur_ready, t + 1)
                v = xx[:, 0:NM * B].rearrange("p (i j b) -> p i j b", i=K, b=B)
                for s in range(2):
                    h = hblur[s * C:(s + 1) * C]
                    a, n = h[:, 0:K, 0:K], h[:, K:0:-1, K:0:-1]
                    dve.tensor_tensor(v[0:C, :, :, t * 2 + s], a, n, ALU.add)
                    last = dve.tensor_tensor(v[C:2 * C, :, :, t * 2 + s], a, n, ALU.subtract)
                last.then_inc(xx_ready, 1)
                dve.wait_ge(xx_ready, t + 1)

            dve.memset(xx[:, NM * B:], 0.0)
            dve.memset(hbuf[:, :, :], 0.0).then_inc(hbuf_zeroed, 1)
            dve.wait_ge(hbuf_zeroed, 1)
            n_first, n_mid = len(taps(True, False)), len(taps(False, False))
            spread(0, 0, 0)
            spread(1, 1, n_first)
            with dve.Fori(2, BP - 1) as i:
                spread(i, 1, i * n_mid + (n_first - n_mid))
                sums(i - 2)
            spread(BP - 1, 2, n_first + (BP - 2) * n_mid)
            for t in range(BP - 3, BP):
                sums(t)
            for n, (p, g) in enumerate(TURNS):
                b0, b1 = PARTS[p]
                dve.wait_ge(turn_full, n + 1)
                dve.tensor_copy(turned[:, g, b0:b1, :], bank[0:MT, n % 4, 0:(b1 - b0) * C].rearrange(
                    "p (b c) -> p b c", b=b1 - b0)).then_inc(turn_out, 1)

            def yr_evac(b, ts):
                for t in ts:
                    dve.wait_ge(u_out, 3 * b + t + 1)
                    src = bank[:, Y0_BANK[t], 0:JB * 2 * NEY].rearrange("p (j s e) -> p j s e", j=JB, s=2)
                    dst = yr[:, E0:E1, :].rearrange("p e (s j) -> p j s e", s=2)[:, t * JB:(t + 1) * JB]
                    if t > 0:
                        last = dve.tensor_copy(dst, src)
                    else:
                        dve.tensor_copy(dst[:, 1:], src[:, 1:])
                        dve.tensor_copy(dst[:, 0, 1], src[:, 0, 1])
                        last = dve.tensor_scalar(dst[:, 0, 0], src[:, 0, 0], B2, None, ALU.add)
                    last.then_inc(yr_out, 1)

            def u_rest(b, k):
                dve.wait_ge(u_hi_ready, b + 1)
                part = slice(12 * k + (k > 0), 12 * k + 13)
                dve.tensor_tensor(u_lo[:, part, :], u[:, part, :], u_hi[:, part, :].bitcast(F32),
                                  ALU.subtract).then_inc(u_lo_ready, 1)

            def prelu1(b, j):
                dve.wait_ge(neg1_ready, G * b + j + 1)
                if j > 0 or not isinstance(b, int):
                    dve.wait_ge(v_ready, G * b + j)
                    dve.wait_ge(v1_ready, G * b + j)
                dve.scalar_tensor_tensor(act_f[:, :, 1:1 + N], neg1[:, :].rearrange("p (e h) -> p e h", e=4), C1,
                                         bank[:, Z1_BANK, :].rearrange("p (e h) -> p e h", e=4),
                                         ALU.mult, ALU.add).then_inc(act_ready, 1)
                dve.wait_ge(act_ready, G * b + j + 1)
                dve.tensor_tensor(v_f[:, :, 1, :], act_f[:, :, 1:1 + N:2], act_f[:, :, 2:2 + N:2],
                                  ALU.add).then_inc(v1_ready, 1)

            def lo(b, j):
                dve.wait_ge(v_hi_ready, G * b + j + 1)
                at = 4 * (j % 3)
                last = dve.tensor_tensor(v_lo[:, at:at + 4], v_f[:, :, :, :], v_hi[:, at:at + 4].bitcast(F32), ALU.subtract)
                if j % 3 == 0:
                    last = dve.tensor_tensor(v_lo[:, VS], v_f[:, 0], v_hi[:, VS].bitcast(F32), ALU.subtract)
                last.then_inc(v_lo_ready, 1)

            def yt_evac(b, t):
                dve.wait_ge(yt_full, 3 * b + t + 1)
                dve.tensor_copy(yt[:, 4 * t:4 * t + 4, :], bank[0:3 * NP, Y_BANK[t], :].rearrange(
                    "p (q c) -> p q c", q=4)).then_inc(yt_out, 1)

            def yt_rest(b, t):
                dve.wait_ge(yt_hi_ready, 3 * b + t + 1)
                part = slice(4 * t, 4 * t + 4)
                dve.tensor_tensor(yt_lo[:, part, :], yt[:, part, :], yt_hi[:, part, :].bitcast(F32),
                                  ALU.subtract).then_inc(yt_lo_ready, 1)

            def sum2(b, g):
                dve.wait_ge(pq_ready, G * b + g + 1)
                dve.wait_ge(conv_full, G * b + g + 1)
                dve.wait_ge(cols_out, G * b + g + G)
                dve.tensor_tensor(y2[:, :].rearrange("p (e h s) -> p e s h", e=4, s=2), pq[:, :, :, :],
                                  bank[:, A_BANK[g % 3], :].rearrange("p (e s h) -> p e s h", e=4, s=2),
                                  ALU.add).then_inc(y2_ready, 1)

            def columns(b, g):
                dve.wait_ge(neg2_ready, G * b + g + 1)
                if g == 0:
                    dve.wait_ge(stored, 16 * (b + 1))
                e = 4 * g + 1
                runs = [(e, 4)] if g != 4 else [(e, 1), (e + 2, 2)]
                for e0, ne in runs:
                    w0 = 2 * e0 + 92 if e0 < EPAD else 2 * (e0 - EPAD - 1)
                    q = (e0 - e) * N
                    for par in range(2):
                        rows = slice(par * C, (par + 1) * C)
                        for half in range(2):
                            cols = slice(half * 64, half * 64 + 64)
                            sneg, spos = (v[rows, q:q + ne * N].rearrange("p (e h) -> p e h", e=ne)[:, :, cols]
                                          for v in (neg2, y2))
                            dst = obuf[half * C:(half + 1) * C, b % 2, :, w0 + par:w0 + par + 2 * ne - 1:2]
                            last = dve.scalar_tensor_tensor(dst.rearrange("p h e -> p e h"), sneg,
                                                            C2[rows, :], spos, ALU.mult, ALU.add)
                last.then_inc(cols_out, 1)

            def step(b, g, more):
                if g > 0:
                    columns(b, g - 1)
                if 0 <= g + LA - 1 < more:
                    lo(b, g + LA - 1)
                if g in (0, G):
                    yt_evac(b + g // G, TURN_Y_AT[0])
                elif g in TURN_Y_AT and more > G:
                    yt_evac(b + 1, TURN_Y_AT[g])
                if g + LA < more:
                    prelu1(b, g + LA)
                if g in YT_REST_AT:
                    yt_rest(b, YT_REST_AT[g])
                elif g == G - 1 and more > G:
                    yt_rest(b + 1, 0)
                if g >= 0:
                    sum2(b, g)

            yr_evac(0, range(3))
            for p in range(len(PARTS)):
                dve.wait_ge(modes_stored[p], 64)
            dve.memset(act_f[:, :, 0:1], 0.0)
            dve.memset(act_f[:, :, HP - 1:HP], 0.0).then_inc(act_zeroed, 1)
            dve.wait_ge(act_zeroed, 1)
            for k in range(ZK):
                u_rest(0, k)
            yt_evac(0, 0)
            yt_evac(0, 1)
            yt_rest(0, 0)
            for g in range(-LA, 0):
                step(0, g, 2 * G)
            dve.wait_ge(v_lo_ready, 1)
            dve.tensor_copy(v_lo[:, VS + 1], v_lo[:, 0])
            dve.tensor_copy(v_hi[:, VS + 1], v_hi[:, 0]).then_inc(kept, 1)
            step(0, 0, 2 * G)
            with dve.Fori(0, B - 1) as b:
                yr_evac(b + 1, INVERSE_AT[0])
                for g in range(1, G + 1):
                    step(b, g, 2 * G)
                    if g == 1:
                        yr_evac(b + 1, INVERSE_AT[1])
                    elif U_SPLIT_AT <= g < U_SPLIT_AT + ZK:
                        u_rest(b + 1, g - U_SPLIT_AT)
            for g in range(1, G):
                if g == G - 2:
                    dve.wait_ge(kept, 1)
                    dve.tensor_copy(v_lo[:, VS], v_lo[:, VS + 1])
                    dve.tensor_copy(v_hi[:, VS], v_hi[:, VS + 1]).then_inc(wrapped, 1)
                step(B - 1, g, G)
            columns(B - 1, G - 1)

        @block.tensor
        def _(pe):
            pe.wait_ge(fwd_in, 16)

            def forward(i):
                for c in range(CPP):
                    s = c % XR
                    pe.wait_ge(x_in[s], 32 * (i * (CPP // XR) + c // XR + 1))
                    for half in range(CH // GI):
                        gi = c * (CH // GI) + half
                        if gi >= 4:
                            pe.wait_ge(rows_out, GPP * i + gi - 3)
                        for q in range(GI):
                            last = pe.matmul(bank[:, gi % 4, q * NF:q * NF + WIDE], xbuf[:, s, half * GI + q, :],
                                             fwd_sb[:, :], start=True, stop=True)
                        last.then_inc(rows_full, 1)
                pe.wait_ge(consts_in, 16 * NC_CONST)
                pe.wait_ge(rows_out, GPP * (i + 1))
                pe.wait_ge(modes_out, i + 1)
                for s in range(2):
                    for e in range(KE):
                        for f in range(2):
                            at = (f * KE + e) * KE
                            last = pe.matmul(bank[s * C:(s + 1) * C, 4, e * KE:e * KE + HALF],
                                             tbuf[:, s * C:(s + 1) * C, f * K + e % K],
                                             f2_sb[:, at:at + HALF], start=f == 0, stop=f == 1)
                last.then_inc(modes_full, 1)

            with pe.Fori(0, BP) as i:
                forward(i)
            pe.wait_ge(xx_ready, BP)
            with pe.Fori(0, NMC // WR) as q:
                part = xx[:, bass.ds(q * (WR * MC * B), WR * MC * B + HALF - B)]
                for s in range(WR):
                    pe.wait_ge(w_in[s], 16 * (q + 1))
                    if s >= 2:
                        pe.wait_ge(mix_out, q * WR + s - 1)
                    for m in range(MC):
                        last = pe.matmul(bank[0:C, 6 + s % 2, m * B:m * B + HALF], wbuf[:, s, m, :],
                                         part[:, (s * MC + m) * B:(s * MC + m) * B + HALF], start=True, stop=True)
                    last.then_inc(mix_full, 1)
                pe.wait_ge(mix_out, q * WR + WR)
            for n, (p, g) in enumerate(TURNS):
                b0, b1 = PARTS[p]
                if n >= 4:
                    pe.wait_ge(turn_out, n - 3)
                for b in range(b0, b1):
                    q = b - b0
                    wide = WIDE if q < 7 else C
                    last = pe.matmul(bank[0:MT, n % 4, q * C:q * C + wide],
                                     mixed[:, b, g * MT:(g + 1) * MT], cblur_sb[:, 0:wide],
                                     start=True, stop=True)
                last.then_inc(turn_full, 1)

            def inverse_w(b, ts):
                for t in ts:
                    if t == 0:
                        pe.wait_ge(yin_in, 64 * (b + 1))
                        if not isinstance(b, int):
                            pe.wait_ge(z_out, 9 * b)
                    elif t == 1:
                        if not isinstance(b, int):
                            pe.wait_ge(yt_out, 3 * b)
                    else:
                        pe.wait_ge(yr_out, 3 * b + 1)
                    for q in range(JB):
                        wide = WIDE if q < JB - 1 else 2 * NEY
                        last = pe.matmul(bank[:, Y0_BANK[t], q * 2 * NEY:q * 2 * NEY + wide],
                                         yin[:, t * JB + q, :], ytab_sb[:, 0:wide], start=True, stop=True)
                    last.then_inc(y_full, 1)

            def conv1(b, ns):
                for n in ns:
                    k, kh = n // 3, n % 3
                    if n == 0:
                        pe.wait_ge(yr_out, 3 * b + 3)
                        pe.wait_ge(u_hi_ready, b + 1)
                    if kh == 0:
                        pe.wait_ge(u_lo_ready, ZK * b + k + 1)
                    if n == 8:
                        pe.wait_ge(yt_out, 3 * b + 2)
                    elif n >= 2:
                        pe.wait_ge(z_out, 9 * b + Z_PREV[n])
                    terms = [(w, v, t) for t in range(2) for w, v in ((w_hi[0], u_hi), (w_hi[0], u_lo), (w_lo[0], u_hi))]
                    for m, (w, v, t) in enumerate(terms):
                        last = pe.matmul(bank[:, Z_BANK[n], 0:12 * NP], w[:, 2 * kh + t, :],
                                         v[:, 12 * k + t:12 * k + t + 12, :], start=m == 0, stop=m == len(terms) - 1)
                    last.then_inc(z_full, 1)

            def turn_z(b, j):
                pe.wait_ge(z_out, 9 * b + 3 * (j // 3) + 3)
                if j > 0 or not isinstance(b, int):
                    pe.wait_ge(zt_out, G * b + j)
                for q in range(4):
                    last = pe.transpose(bank[0:3 * NP, TURN_BANK, q * 128:(q + 1) * 128],
                                        z[:, 4 * (j % G) + q, :], ident_sb[:, :])
                last.then_inc(zt_full, 1)

            def turn_y(b, t):
                if t == 1:
                    pe.wait_ge(yt_out, 3 * b + 1)
                else:
                    pe.wait_ge(z_out, 9 * b + (5 if t == 0 else 8))
                for q in range(4):
                    e = E0 - 1 + 3 * (4 * t + q)
                    last = pe.transpose(bank[0:3 * NP, Y_BANK[t], q * 128:(q + 1) * 128],
                                        yr[:, e:e + 3, :], ident_sb[:, :])
                last.then_inc(yt_full, 1)

            def lift_rows(b, j):
                pe.wait_ge(zt_out, G * b + j + 1)
                if j > 0 or not isinstance(b, int):
                    pe.wait_ge(act_ready, G * b + j)
                for q in range(4):
                    last = pe.matmul(bank[:, Z1_BANK, q * N:(q + 1) * N], zt[:, q * 128:(q + 1) * 128],
                                     lift_sb[:, :], start=True, stop=True)
                last.then_inc(z1_full, 1)

            def conv2(b, g, more, part):
                halves = {m: bank[:, bk, :].rearrange("p (e s h) -> p e s h", e=4, s=2)[:, :, s]
                          for m, bk, s in ((0, A_BANK[g % 3], 0), (3, A_BANK[g % 3], 1), (1, B_BANK, 0), (2, B_BANK, 1))}

                def products(ms, t):
                    at = 4 * (g % 3) + t
                    for m in ms:
                        for k, (w, v) in enumerate(((w_hi[1], v_hi), (w_hi[1], v_lo), (w_lo[1], v_hi))):
                            last = pe.matmul(halves[m], w[:, 2 * m + t, :], v[:, at:at + 4, m, :],
                                             start=t == 0 and k == 0 and m == ms[0],
                                             stop=t == 1 and k == 2 and m == 2)
                    return last

                if part == 1:
                    pe.wait_ge(y2_ready, G * b + g + 1)
                    for t in range(2):
                        products((0, 3), t)
                    if g % 3 == 0:
                        pe.wait_ge(yt_lo_ready, 3 * b + g // 3 + 1)
                    first, end = 4 * g, 4 * g + 4
                    for turn in range(first // 3, (end + 2) // 3):
                        n0, n1 = max(first, 3 * turn), min(end, 3 * turn + 3)
                        dst = bank[:, A_BANK[g % 3], (n0 - first) * N:(n1 - first) * N]
                        terms = [(yt, rowfun_sb)] if n1 - n0 == 1 else [(yt_hi, rowfun_hi), (yt_lo, rowfun_hi), (yt_hi, rowfun_lo)]
                        for k, (v, fun) in enumerate(terms):
                            last = pe.matmul(dst, v[:, turn, :], fun[:, n0 - 3 * turn:n1 - 3 * turn, :].rearrange("p e h -> p (e h)"),
                                             start=False, stop=n1 == end and k == len(terms) - 1)
                    last.then_inc(conv_full, 1)
                    return
                pe.wait_ge(v_lo_ready, G * b + g + 1)
                pe.wait_ge(m12_out, G * b + g + 1)
                products((1, 2), 0)
                if g + 1 < more:
                    pe.wait_ge(v_lo_ready, G * b + g + 2)
                else:
                    pe.wait_ge(wrapped, 1)
                products((1, 2), 1).then_inc(m12_full, 1)

            def step(b, g, more):
                if g >= 0:
                    conv2(b, g, more, 0)
                if g == 0:
                    turn_y(b, TURN_Y_AT[0])
                elif g in TURN_Y_AT and more > G:
                    turn_y(b + 1, TURN_Y_AT[g])
                if g + LA < more:
                    lift_rows(b, g + LA)
                if g + LA + 1 < more:
                    turn_z(b, g + LA + 1)
                if g >= 0:
                    conv2(b, g, more, 1)

            pe.wait_ge(w_split, 2)
            inverse_w(0, range(3))
            conv1(0, range(6))
            turn_y(0, 0)
            conv1(0, (6,))
            turn_y(0, 1)
            conv1(0, (7, 8))
            turn_z(0, 0)
            for g in range(-LA, 0):
                step(0, g, 2 * G)
            with pe.Fori(0, B - 1) as b:
                for g in range(G):
                    step(b, g, 2 * G)
                    inverse_w(b + 1, INVERSE_AT.get(g, ()))
                    conv1(b + 1, CONV1_AT.get(g, ()))
            for g in range(G):
                step(B - 1, g, G)


def tables():
    import numpy as np

    r = np.arange(-R, R + 1, dtype=np.float32)
    kern = np.exp(-0.5 * (r / 1.0) ** 2)
    kern = (kern / kern.sum()).astype(np.float32).astype(np.float64)

    def blur_matrix(n):
        m = np.zeros((n, n))
        for i in range(n):
            for d in range(2 * R + 1):
                m[i, min(max(i + d - R, 0), n - 1)] += kern[d]
        return m

    pos = np.arange(N)
    ang = 2 * np.pi / N
    k = np.arange(K)
    ke = np.arange(KE) % K
    fwd = np.concatenate([np.cos(ang * pos[:, None] * k), np.sin(ang * pos[:, None] * k)], 1)
    cw, sw = np.cos(ang * pos[:, None] * ke), np.sin(ang * pos[:, None] * ke)
    cw1, sw1 = np.cos(ang * (pos[:, None] + 1) * ke), np.sin(ang * (pos[:, None] + 1) * ke)
    ca, sa = np.cos(ang * ke)[None, :, None], np.sin(ang * ke)[None, :, None]
    f2 = np.stack([cw[:, None] - sa * cw1[:, None] - ca * sw1[:, None],
                   -sw[:, None] - ca * cw1[:, None] + sa * sw1[:, None]], 1)
    bb, mb = np.zeros((2, C, 3, 10)), blur_matrix(B)
    for edge, i in enumerate((0, 3, BP - 1)):
        for d in range(-2, 3):
            if 0 <= i + d < BP:
                for s in range(2):
                    bb[s, :, edge, d + 2] = mb[2 * (i + d) + s, 2 * i + s]
                    bb[s, :, edge, d + 7] = mb[2 * (i + d) + s, 2 * i + 1 - s]
    bb = bb.reshape(128, 30)
    cb = blur_matrix(C).T
    blur = blur_matrix(N)
    j = np.arange(KE)
    rc, rs = blur @ np.cos(ang * pos[:, None] * j), blur @ np.sin(ang * pos[:, None] * j)
    funs = np.concatenate([rc, rs], 1).T
    lift = np.zeros((3, NP, N))
    lift[0, :, 1:] = funs[:, :-1]
    lift[1] = funs
    lift[2, :, :-1] = funs[:, 1:]
    rowfun = np.zeros((3, NP, 3, N))
    for q in range(3):
        rowfun[q, :, q] = np.concatenate([funs[:, 0::2], funs[:, 1::2]], 1)
    rowfun = rowfun.reshape(3 * NP, 3, N)
    keep = ((pos < WLO) | (pos >= WHI)).astype(np.float64)
    scale = 0.5 / (N * N)
    rc, rs = rc * keep[:, None] * scale, rs * keep[:, None] * scale
    yt = np.zeros((4 * K, 2, NEY))
    for e in range(E0, E1):
        if e == EPAD:
            continue
        for par in range(2):
            w = (2 * e + 92 if e < EPAD else 2 * (e - EPAD - 1)) + par
            at = 2 * K * par
            yt[at:at + K, 0, e - E0] = rc[w, :K]
            yt[at + K:at + 2 * K, 0, e - E0] = -rs[w, 1:]
            yt[at:at + K, 1, e - E0] = -rs[w, :K]
            yt[at + K:at + 2 * K, 1, e - E0] = -rc[w, 1:]
    fwd = np.pad(fwd, ((0, 0), (0, WIDE - NF)))
    f2 = np.pad(f2.reshape(N, 2 * KE * KE), ((0, 0), (0, HALF)))
    cb = np.pad(cb, ((0, 0), (0, WIDE - C)))
    out = dict(fwd=fwd, f2tab=f2, bblur=bb, cblur=cb, ytab=np.pad(yt.reshape(4 * K, 2 * NEY), ((0, 0), (0, WIDE - 2 * NEY))),
               lift=lift.reshape(3 * NP, N), rowfun=rowfun, ident=np.eye(128))
    return {n: np.ascontiguousarray(a.astype(np.float32)) for n, a in out.items()}


def kernel(**inputs):
    import numpy as _np
    import concourse.bacc as _bacc
    from concourse import mybir as _mybir
    from concourse.bass_utils import run_bass_kernel_spmd as _run

    a = {n: _np.asarray(v) for n, v in inputs.items()}
    w0 = a["L0_conv_w1"]
    neg = (-_np.arange(K)) % K
    w0n = w0[:, :, neg][:, :, :, neg]
    wmix = _np.concatenate([w.transpose(0, 2, 3, 1).reshape(C, NM, C) for w in (w0, w0n)], 0)
    wconv = _np.zeros((2, 3, 2, 2, C, 2, C), _np.float32)
    for l, name in enumerate(("L1_conv_w1", "L1_conv_w2")):
        wt = a[name].transpose(2, 3, 1, 0)
        for t in range(2):
            for pi in range(2):
                for po in range(2):
                    kw = 2 * t + pi - po
                    if 0 <= kw <= 2:
                        wconv[l, :, t, pi, :, po, :] = wt[:, kw]
    wconv = wconv.transpose(3, 4, 0, 1, 2, 5, 6).reshape(128, 2, 6, 128)
    cols = [a[f"L1_conv_bn{l}_{p}"] for l in range(3) for p in "gbmv"] + [a["L1_conv_prelu1_a"], a["L1_conv_prelu2_a"]]
    pcol = _np.tile(_np.stack(cols, 1), (2, 1))
    rows = _np.stack([a["L1_conv_bn1_g"], a["L1_conv_bn1_v"], a["L1_conv_bn2_g"], a["L1_conv_bn2_v"]])
    prow = _np.tile(_np.tile(rows, (1, 2))[None], (128, 1, 1))

    host = dict(x=a["x"], wmix=wmix, wconv=wconv, pcol=pcol, prow=prow, **tables())
    nc = _bacc.Bacc("TRN2", target_bir_lowering=False, num_devices=1)
    arrays, args = {}, {}
    for name, v in host.items():
        v = _np.ascontiguousarray(v)
        arrays[f"in_{name}_dram"] = v
        args[name] = nc.dram_tensor(f"in_{name}_dram", v.shape, _mybir.dt.from_np(v.dtype), kind="ExternalInput").ap()
    args["out"] = nc.dram_tensor("out_0_dram", (B, C, N, N), F32, kind="ExternalOutput").ap()
    conv_seq_kernel(nc, **args)
    r = _run(nc, [arrays], core_ids=[0])
    return r.results[0]["out_0_dram"]
```
